# Optimizing a Trainium2 kernel written in Bass

```python
import numpy as np
import jax
import jax.numpy as jnp

def _softmax(x, axis=-1):
    return jax.nn.softmax(x, axis=axis)

def _gelu(x):
    return jax.nn.gelu(x, approximate=True)

def _silu(x):
    return jax.nn.silu(x)

def _sigmoid(x):
    return jax.nn.sigmoid(x)

def _layernorm(x, axis=-1, eps=1e-05):
    m = jnp.mean(x, axis=axis, keepdims=True)
    v = jnp.var(x, axis=axis, keepdims=True)
    return (x - m) / jnp.sqrt(v + eps)

def _scatter_add(tgt, idx, src, axis=0):
    return tgt.at[idx].add(src)

def _segment_sum(src, seg, n):
    return jax.ops.segment_sum(src, seg, n)
kernel_name = 'mk_seq_postln_d1_jaxref_r8_5ef821'

def setup_inputs(seed: int=0):
    np.random.seed(seed)
    _w = jnp.asarray

    def _L0_attn_setup():
        import jax, jax.numpy as jnp
        import numpy as np
        B, L, E = (2, 256, 256)
        NUM_HEADS = 16
        NUM_KV_HEADS = 2
        HEAD_DIM = E // NUM_HEADS
        THETA = 10000.0

        def apply_rope(x, theta=THETA):
            D = x.shape[-1]
            half = D // 2
            inv_freq = theta ** (-jnp.arange(half, dtype=jnp.float32) / half)
            pos = jnp.arange(x.shape[1], dtype=jnp.float32)
            ang = pos[:, None] * inv_freq[None, :]
            cos = jnp.cos(ang)[None, :, None, :].astype(x.dtype)
            sin = jnp.sin(ang)[None, :, None, :].astype(x.dtype)
            x1, x2 = (x[..., :half], x[..., half:])
            return jnp.concatenate([x1 * cos - x2 * sin, x2 * cos + x1 * sin], axis=-1)
        key = jax.random.key(seed)
        ks = jax.random.split(key, 8)
        s = 0.02
        return {'x': jax.random.normal(ks[0], (B, L, E), dtype=jnp.float32), 'wq': jax.random.normal(ks[1], (NUM_HEADS * HEAD_DIM, E), dtype=jnp.float32) * s, 'wk': jax.random.normal(ks[2], (NUM_KV_HEADS * HEAD_DIM, E), dtype=jnp.float32) * s, 'wv': jax.random.normal(ks[3], (NUM_KV_HEADS * HEAD_DIM, E), dtype=jnp.float32) * s, 'wo': jax.random.normal(ks[4], (E, NUM_HEADS * HEAD_DIM), dtype=jnp.float32) * s, 'bq': jax.random.normal(ks[5], (NUM_HEADS * HEAD_DIM,), dtype=jnp.float32) * s, 'bk': jax.random.normal(ks[6], (NUM_KV_HEADS * HEAD_DIM,), dtype=jnp.float32) * s, 'bv': jax.random.normal(ks[7], (NUM_KV_HEADS * HEAD_DIM,), dtype=jnp.float32) * s}
    _L0_attn_in = _L0_attn_setup()

    def _L0_ffn_setup():
        import jax, jax.numpy as jnp
        import numpy as np
        E, H, I = (8, 256, 512)
        TOP_K = 1
        B, S = (1, 256)
        key = jax.random.key(seed)
        ks = jax.random.split(key, 7)
        std = 0.02
        return {'hidden_states': jax.random.normal(ks[0], (B, S, H), dtype=jnp.float32), 'router_w': jax.random.normal(ks[1], (E, H), dtype=jnp.float32) * std, 'gate_up_proj': jax.random.normal(ks[2], (E, H, 2 * I), dtype=jnp.float32) * std, 'down_proj': jax.random.normal(ks[3], (E, I, H), dtype=jnp.float32) * std, 'shared_gate_w': jax.random.normal(ks[4], (H, I), dtype=jnp.float32) * std, 'shared_up_w': jax.random.normal(ks[5], (H, I), dtype=jnp.float32) * std, 'shared_down_w': jax.random.normal(ks[6], (I, H), dtype=jnp.float32) * std}
    _L0_ffn_in = _L0_ffn_setup()
    _d = {'L0_attn_x': _L0_attn_in['x'], 'L0_attn_wq': _L0_attn_in['wq'], 'L0_attn_wk': _L0_attn_in['wk'], 'L0_attn_wv': _L0_attn_in['wv'], 'L0_attn_wo': _L0_attn_in['wo'], 'L0_attn_bq': _L0_attn_in['bq'], 'L0_attn_bk': _L0_attn_in['bk'], 'L0_attn_bv': _L0_attn_in['bv'], 'L0_ffn_router_w': _L0_ffn_in['router_w'], 'L0_ffn_gate_up_proj': _L0_ffn_in['gate_up_proj'], 'L0_ffn_down_proj': _L0_ffn_in['down_proj'], 'L0_ffn_shared_gate_w': _L0_ffn_in['shared_gate_w'], 'L0_ffn_shared_up_w': _L0_ffn_in['shared_up_w'], 'L0_ffn_shared_down_w': _L0_ffn_in['shared_down_w']}
    _x0 = _d['L0_attn_x']
    _d['L0_attn_x'] = jax.random.normal(jax.random.fold_in(jax.random.key(seed), 1), (4, 256, 256), dtype=_x0.dtype)
    del _x0
    return _d

def reference(L0_attn_x, L0_attn_wq, L0_attn_wk, L0_attn_wv, L0_attn_wo, L0_attn_bq, L0_attn_bk, L0_attn_bv, L0_ffn_router_w, L0_ffn_gate_up_proj, L0_ffn_down_proj, L0_ffn_shared_gate_w, L0_ffn_shared_up_w, L0_ffn_shared_down_w):

    def _L0_attn_ref(x, wq, wk, wv, wo, bq, bk, bv):
        import jax, jax.numpy as jnp
        import numpy as np
        B, L, E = (2, 256, 256)
        NUM_HEADS = 16
        NUM_KV_HEADS = 2
        HEAD_DIM = E // NUM_HEADS
        THETA = 10000.0

        def apply_rope(x, theta=THETA):
            D = x.shape[-1]
            half = D // 2
            inv_freq = theta ** (-jnp.arange(half, dtype=jnp.float32) / half)
            pos = jnp.arange(x.shape[1], dtype=jnp.float32)
            ang = pos[:, None] * inv_freq[None, :]
            cos = jnp.cos(ang)[None, :, None, :].astype(x.dtype)
            sin = jnp.sin(ang)[None, :, None, :].astype(x.dtype)
            x1, x2 = (x[..., :half], x[..., half:])
            return jnp.concatenate([x1 * cos - x2 * sin, x2 * cos + x1 * sin], axis=-1)
        b, l, _ = x.shape
        Hq, Hkv, Dh = (NUM_HEADS, NUM_KV_HEADS, HEAD_DIM)
        G = Hq // Hkv
        scale = 1.0 / Dh ** 0.5
        q = (x @ wq.T + bq).reshape(b, l, Hq, Dh)
        k = (x @ wk.T + bk).reshape(b, l, Hkv, Dh)
        v = (x @ wv.T + bv).reshape(b, l, Hkv, Dh)
        q = apply_rope(q)
        k = apply_rope(k)
        q = q.transpose(0, 2, 1, 3).reshape(b, Hkv, G, l, Dh).astype(jnp.float32)
        k = k.transpose(0, 2, 1, 3).astype(jnp.float32)
        v = v.transpose(0, 2, 1, 3).astype(jnp.float32)
        scores = jnp.einsum('bhgqd,bhkd->bhgqk', q, k) * scale
        causal = jnp.tril(jnp.ones((l, l), dtype=bool))
        scores = jnp.where(causal[None, None, None, :, :], scores, -jnp.inf)
        attn = jax.nn.softmax(scores, axis=-1)
        out = jnp.einsum('bhgqk,bhkd->bhgqd', attn, v)
        out = out.reshape(b, Hq, l, Dh).transpose(0, 2, 1, 3).reshape(b, l, Hq * Dh)
        out = out.astype(x.dtype)
        return out @ wo.T

    def _L0_ffn_ref(hidden_states, router_w, gate_up_proj, down_proj, shared_gate_w, shared_up_w, shared_down_w):
        import jax, jax.numpy as jnp
        import numpy as np
        E, H, I = (8, 256, 512)
        TOP_K = 1
        B, S = (1, 256)
        orig_shape = hidden_states.shape
        x = hidden_states.reshape(-1, H)
        T = x.shape[0]
        logits = x @ router_w.T
        top_vals, top_idx = jax.lax.top_k(logits, TOP_K)
        scores = jnp.full_like(logits, -jnp.inf)
        scores = scores.at[jnp.arange(T)[:, None], top_idx].set(top_vals)
        scores = jax.nn.sigmoid(scores.astype(jnp.float32)).astype(logits.dtype)
        xr = x[None, :, :] * scores.T[:, :, None]
        gate_up = jnp.einsum('eth,ehf->etf', xr, gate_up_proj)
        gate, up = jnp.split(gate_up, 2, axis=-1)
        routed = jnp.einsum('etf,efh->eth', up * jax.nn.silu(gate), down_proj)
        routed_sum = routed.sum(axis=0)
        shared = jax.nn.silu(x @ shared_gate_w) * (x @ shared_up_w) @ shared_down_w
        return (shared + routed_sum).reshape(orig_shape)
    x = L0_attn_x
    x = _layernorm(x + _L0_attn_ref(x, L0_attn_wq, L0_attn_wk, L0_attn_wv, L0_attn_wo, L0_attn_bq, L0_attn_bk, L0_attn_bv), axis=-1)
    x = _layernorm(x + _L0_ffn_ref(x, L0_ffn_router_w, L0_ffn_gate_up_proj, L0_ffn_down_proj, L0_ffn_shared_gate_w, L0_ffn_shared_up_w, L0_ffn_shared_down_w), axis=-1)
    return x

_drawn_inputs = setup_inputs


def setup_inputs(seed=0):
    import zlib

    import numpy as np

    out = dict(_drawn_inputs(seed))
    spreads = {}
    factors = {'L0_attn_wq': 8.0,
     'L0_attn_wk': 8.0,
     'L0_attn_wv': 3.503,
     'L0_attn_wo': 3.17,
     'L0_attn_bq': 8.0,
     'L0_attn_bk': 8.0,
     'L0_attn_bv': 8.0,
     'L0_ffn_router_w': 6.582,
     'L0_ffn_gate_up_proj': 6.14,
     'L0_ffn_down_proj': 6.122,
     'L0_ffn_shared_gate_w': 8.0,
     'L0_ffn_shared_up_w': 8.0,
     'L0_ffn_shared_down_w': 8.0}
    for name, (base, spread) in spreads.items():
        noise = np.random.default_rng([zlib.crc32(name.encode()), seed]).standard_normal(out[name].shape)
        drawn = base * np.exp(spread * noise) if base else spread * noise
        out[name] = jnp.asarray(drawn.astype(out[name].dtype))
    for name, factor in factors.items():
        out[name] = (out[name] * factor).astype(out[name].dtype)
    return out
```

```python
import numpy as np
import concourse.bass as bass
from concourse import mybir
from contextlib import ExitStack

FP32 = mybir.dt.float32
FP32R = mybir.dt.float32r
BF16 = mybir.dt.bfloat16
U32 = mybir.dt.uint32
I32 = mybir.dt.int32
ALU = mybir.AluOpType
ACT = mybir.ActivationFunctionType
AX = mybir.AxisListType

P = 128
B, L, E = 4, 256, 256
T = B * L
NT = T // P
KE = E // P
HQ, HKV, D = 16, 2, 16
HALF = D // 2
HR = HQ + HKV
NQKV = (HQ + 2 * HKV) * D
NX, F = 8, 512
KF = F // P
TT = L // P
PAIRS = HQ // 2
NP = B * PAIRS
NG = NP // 2
GB = HQ // 4
CAP = 256
NSLOT = NX * CAP
THETA = 10000.0
EPS = 1e-5
MASKED = -1.0e30
WSET = KE * 2 * F + KF * E
NSETS = 1 + NX
SHARED_BLOCKS = T // CAP
NB = SHARED_BLOCKS + NX
RAW = 3


def misc_uses():
    slots = [[] for _ in range(NP + 1)]
    for b in range(B):
        at = PAIRS * b
        if b + 1 < B:
            slots[at] += [("proj", b + 1, 0)]
            slots[at + 1] += [("proj", b + 1, 1)]
            slots[at + 3] += [("qT", b + 1, 0)]
            slots[at + 4] += [("qT", b + 1, 1), ("qT", b + 1, 2)]
            slots[at + 5] += [("qT", b + 1, 3), ("kT", b + 1, 0)]
        if b:
            slots[at + 1] += [("otr", b - 1, 0)]
            slots[at + 2] += [("otr", b - 1, 1)]
            slots[at + 3] += [("onT", b - 1, 0)]
            slots[at + 6] += [("wo", b - 1, 0)]
    first = [("proj", 0, 0), ("proj", 0, 1)] + [("qT", 0, i) for i in range(4)] + [("kT", 0, 0)]
    slots[NP] = [("otr", B - 1, 0), ("otr", B - 1, 1), ("onT", B - 1, 0), ("wo", B - 1, 0)]
    order = first + [u for s in slots for u in s]
    return first, slots, {u: i for i, u in enumerate(order)}


def set_of(block):
    return 0 if block < SHARED_BLOCKS else block - SHARED_BLOCKS + 1


def last_block(s):
    return SHARED_BLOCKS - 1 + s


def part_of(part):
    return slice(0, KE * 2 * F) if part == 0 else slice(KE * 2 * F, WSET)


def half_of(part, second):
    c = part_of(part)
    half = (c.stop - c.start) // 2
    return slice(c.start + second * half, c.start + (second + 1) * half)


def program(nc, x, xT, wqkvT, bqkv, woT, rwT, wgu, wd, swg, swu, swd, cosq, sinq, cf, cb, out):
    first_uses, slot_uses, use_at = misc_uses()
    xs_dram = nc.dram_tensor("xs_dram", (NSLOT, E), FP32).ap()
    ys_dram = nc.dram_tensor("ys_dram", (NSLOT, E), FP32).ap()

    ctx = ExitStack()
    with ctx:
        def sb(name, shape, dt=FP32):
            return ctx.enter_context(nc.sbuf_tensor(name, shape, dt))

        def sem(name):
            return ctx.enter_context(nc.semaphore(name))

        xT_s = sb("xT_s", [P, KE, T])
        wqkv_s = sb("wqkv_s", [P, KE, NQKV])
        bias_s = sb("bias_s", [P, NQKV])
        wo_s = sb("wo_s", [P, KE, E])
        cos_s = sb("cos_s", [P, TT, HR, D])
        sin_s = sb("sin_s", [P, TT, HR, 2, HALF])
        cf_s = sb("cf_s", [P, P + NX])
        cb_s = sb("cb_s", [P, 5 * P], BF16)
        ident = cf_s[:, 0:P]
        expert_no = cf_s[:, P:P + NX]
        ident_b = cb_s[:, 0:P]
        mask2 = cb_s[:, P:3 * P].rearrange("p (a k) -> p a k", a=2)
        earlier = cb_s[:, 3 * P:4 * P]
        ones_b = cb_s[:, 4 * P:5 * P]
        rw_s = sb("rw_s", [P, KE, NX])
        rw_r = sb("rw_r", [P, KE, 2, NX], FP32R)

        qkv = sb("qkv", [P, TT, NQKV])
        rot_c = sb("rot_c", [P, TT, HR, D])
        rot_s = sb("rot_s", [P, TT, HR, 2, HALF])
        rot = sb("rot", [P, TT, HR, D])
        q4 = sb("q4", [P, TT, HQ, 4, D], FP32R)
        k4 = sb("k4", [P, TT, HKV, 4, 2, D], FP32R)
        q4T = sb("q4T", [P, 2, PAIRS, L], FP32R)
        kbd = sb("kbd", [P, 2, HKV, 2, L], FP32R)
        v_s = sb("v_s", [P, 2, TT, HKV, 2 * D])
        negmax = sb("negmax", [P, B, TT, HQ])
        denom = sb("denom", [P, B, TT, HQ])
        rdenom = sb("rdenom", [P, TT, HQ])
        probs = sb("probs", [P, 2, 2, L + P])
        probsT = sb("probsT", [P, 2, 4, L + P])
        oT_s = sb("oT_s", [P, GB, L])
        on = sb("on", [P, TT, HQ, D])
        onT_s = sb("onT_s", [P, TT, KE, P])
        r1 = sb("r1", [P, NT, E])

        stats = sb("stats", [P, NT, 6])
        mv = sb("mv", [P, NT, 2])
        std = sb("std", [P, NT])
        rstd = sb("rstd", [P, NT])
        x1T_h = sb("x1T_h", [P, KE, T], FP32R)
        x1T_l = sb("x1T_l", [P, KE, T], FP32R)
        lg = sb("lg", [P, NT, NX])
        top = sb("top", [P, NT])
        pick = sb("pick", [P, NT, NX])
        first = sb("first", [P, NT])
        onehot = sb("onehot", [P, NT, NX])
        onehot_b = sb("onehot_b", [P, NT, NX], BF16)
        score = sb("score", [P, NT])
        place = sb("place", [P, NT, NX])
        slot_f = sb("slot_f", [P, NT])
        over = sb("over", [P, NT])
        over_b = sb("over_b", [P, NT], BF16)
        over_mask = sb("over_mask", [P, NT, NX])
        n_over_f = sb("n_over_f", [P, 1])
        n_over = sb("n_over", [P, 1], I32)
        slot_u = sb("slot_u", [P, NT], U32)
        base = sb("base", [P, NX])
        x1s = sb("x1s", [P, 2, E])
        zero = sb("zero", [P, E])

        w_raw = sb("w_raw", [P, RAW, WSET])
        w_h = sb("w_h", [P, 2, WSET], FP32R)
        w_l = sb("w_l", [P, 2, WSET], FP32R)
        spare = probsT[:, :, :, :].rearrange("p a h q -> p (a h q)")
        xs, ys = (spare[:, i * 2 * TT * E:(i + 1) * 2 * TT * E].rearrange("p (a t e) -> p a t e", a=2, t=TT)
                  for i in range(2))
        gate, hT = (spare[:, (4 * TT * E + i * 2 * CAP):(4 * TT * E + (i + 1) * 2 * CAP)].rearrange(
            "p (a c) -> p a c", a=2) for i in range(2))
        spare = kbd[:, :, :, :, :].rearrange("p a h j k -> p (a h j k)").rearrange(
            "p (s a k c) -> p s a k c", s=2, a=2, k=KE)
        xsT_h, xsT_l = spare[:, 0], spare[:, 1]
        spare = q4T[:, :, :, :].rearrange("p a u q -> p (a u q)").rearrange(
            "p (s a f c) -> p s a f c", s=2, a=2, f=KF)
        hT_h, hT_l = spare[:, 0], spare[:, 1]
        y_sh = xT_s[:, :, :].rearrange("p k t -> p (k t)").rearrange("p (t e) -> p t e", t=NT)
        back = q4[:, :, :, :, :].bitcast(FP32).rearrange("p a h s d -> p (a h s d)").rearrange(
            "p (t e) -> p t e", t=NT)

        bank = [ctx.enter_context(nc.psum_tensor(f"bank{i}", [P, 512], FP32)) for i in range(8)]
        SCORES, PT, OT, MISC = [0, 2], [4, 5], 6, 7

        masks_f = probs[:, :, :, :].rearrange("p a j q -> p (a j q)")[:, 0:5 * P]
        spare = probs[:, :, :, :].rearrange("p a j q -> p (a j q)")
        xsT_o = spare[:, 0:KE * CAP].rearrange("p (k c) -> p k c", k=KE)
        hT_o = spare[:, KE * CAP:(KE + KF) * CAP].rearrange("p (f c) -> p f c", f=KF)

        ld_c, ld_x, ld_w, ld_r = sem("ld_consts"), sem("ld_x"), sem("ld_wo"), sem("ld_tok")
        raw_in = [sem(f"raw_in{i}") for i in range(RAW)]
        init, masks_ready = sem("init"), sem("masks_ready")
        misc_full, misc_free = sem("misc_full"), sem("misc_free")
        rope_in, rope_sin, rope_sum, q_high, q_low = (
            sem("rope_in"), sem("rope_sin"), sem("rope_sum"), sem("q_high"), sem("q_low"))
        v_ready = sem("v_ready")
        qT_act, qT_dve = sem("qT_act"), sem("qT_dve")
        kT_ready = sem("kT_ready")
        scores_full, max_ready, exp_ready = sem("scores_full"), sem("max_ready"), sem("exp_ready")
        pt_full, pt_ev = sem("pt_full"), [sem("pt_ev0"), sem("pt_ev1")]
        pv_done, o_ev = sem("pv_done"), sem("o_ev")
        on_ready, onT_ready, r1_ready = sem("on_ready"), sem("onT_ready"), sem("r1_ready")
        dve_link = sem("dve_link")
        var_ready, std_ready, x1_ready = sem("var_ready"), sem("std_ready"), sem("x1_ready")
        x1T_full, x1T_high, x1T_low = sem("x1T_full"), sem("x1T_high"), sem("x1T_low")
        rw_ready = sem("rw_ready")
        logits_full, onehot_ready, rank_full = sem("logits_full"), sem("onehot_ready"), sem("rank_full")
        top_ready, score_ready, slot_ready = sem("top_ready"), sem("score_ready"), sem("slot_ready")
        scaled, zeroed = sem("scaled"), sem("zeroed")
        zero_rows = sem("zero_rows")
        scattered = [sem("scattered0"), sem("scattered1")]
        w_high, w_low_dve, w_low_pool = sem("w_high"), sem("w_low_dve"), sem("w_low_pool")
        xs_in = [sem("xs_in0"), sem("xs_in1")]
        xsT_full, xsT_high, xsT_low = sem("xsT_full"), sem("xsT_high"), sem("xsT_low")
        gu_full, gate_ready, h_ready, h_high, h_low = (
            sem("gu_full"), sem("gate_ready"), sem("h_ready"), sem("h_high"), sem("h_low"))
        y_full, y_sh_ready, ys_ready = sem("y_full"), sem("y_sh_ready"), sem("ys_ready")
        ys_out = [sem("ys_out0"), sem("ys_out1")]
        got = [sem(f"got{t}") for t in range(NT)]
        var2, std2, done = sem("var2"), sem("std2"), sem("done")
        stored = sem("stored")
        over_ready, over_full, n_over_ready = sem("over_ready"), sem("over_full"), sem("n_over_ready")
        back_zero = sem("back_zero")
        o_w, o_rows, o_xT_full, o_xT, o_gu, o_gate, o_h, o_y, o_sum = (
            sem("o_weights"), sem("o_rows"), sem("o_xT_full"), sem("o_xT"), sem("o_gate_up"),
            sem("o_gate"), sem("o_h"), sem("o_y"), sem("o_sum"))
        block = ctx.enter_context(nc.Block())

        def gu(par, high, f, k, up):
            w = (w_h if high else w_l)[:, par, 0:KE * 2 * F].rearrange("p (k n) -> p k n", k=KE)
            return w[:, k, up * F + f * P:up * F + (f + 1) * P]

        def down(par, high, f):
            w = (w_h if high else w_l)[:, par, KE * 2 * F:].rearrange("p (f n) -> p f n", f=KF)
            return w[:, f, :]

        def overflow(eng):
            eng.wait_ge(n_over_ready, 1)
            return eng.If(eng.value_load(n_over[0:1, 0:1], min_val=0, max_val=T) > 0)

        @block.sync
        def _(sp):
            sp.dma_start(wqkv_s[:, :, :], wqkvT.rearrange("(k p) n -> p k n", p=P)).then_inc(ld_x, 16)
            xTv = xT.rearrange("(k p) t -> p k t", p=P)
            sp.dma_start(xT_s[:, :, 0:L], xTv[:, :, 0:L]).then_inc(ld_x, 16)
            sp.dma_start(xT_s[:, :, L:T], xTv[:, :, L:T]).then_inc(ld_w, 16)
            sp.dma_start(wo_s[:, :, :], woT.rearrange("(k p) n -> p k n", p=P)).then_inc(ld_w, 16)
            sp.dma_start(r1[:, :, :], x.rearrange("(t p) e -> p t e", p=P)).then_inc(ld_r, 16)
            sp.dma_start(rw_s[:, :, :], rwT.rearrange("(k p) n -> p k n", p=P)).then_inc(ld_r, 16)
            sp.wait_ge(zeroed, 1)
            for e in range(NX):
                for t in range(TT):
                    at = (e * TT + t) * P
                    sp.dma_start(xs_dram[at:at + P, :], zero[:, :]).then_inc(zero_rows, 16)

            def load_set(s):
                if s >= RAW:
                    for split in (w_high, w_low_dve, w_low_pool):
                        sp.wait_ge(split, 2 * (s - RAW) + 2)
                r = w_raw[:, s % RAW, :]
                g, d = r[:, 0:KE * 2 * F].rearrange("p (k n) -> p k n", k=KE), r[:, KE * 2 * F:]
                if s == 0:
                    sp.dma_start(g[:, :, 0:F], swg.rearrange("(k p) n -> p k n", p=P)).then_inc(raw_in[0], 16)
                    sp.dma_start(g[:, :, F:], swu.rearrange("(k p) n -> p k n", p=P)).then_inc(raw_in[0], 16)
                    src = swd
                else:
                    sp.dma_start(g, wgu[s - 1].rearrange("(k p) n -> p k n", p=P)).then_inc(raw_in[s % RAW], 16)
                    src = wd[s - 1]
                sp.dma_start(d.rearrange("p (f n) -> p f n", f=KF),
                             src.rearrange("(f p) n -> p f n", p=P)).then_inc(raw_in[s % RAW], 16)

            for s in range(RAW):
                load_set(s)
            for n in range(SHARED_BLOCKS, NB):
                e = n - SHARED_BLOCKS
                if e == 0:
                    sp.wait_ge(scattered[0], 16 * (NT // 2))
                    sp.wait_ge(scattered[1], 16 * (NT // 2))
                if e >= 2:
                    sp.wait_ge(xsT_full, e - 1)
                sp.dma_start(xs[:, e % 2, :, :],
                             xs_dram[e * CAP:(e + 1) * CAP, :].rearrange("(t p) d -> p t d", p=P)
                             ).then_inc(xs_in[e % 2], 16)
                if e + 2 >= RAW and e + 2 < NSETS:
                    load_set(e + 2)
                if e >= 1:
                    sp.wait_ge(ys_ready, e)
                    sp.dma_start(ys_dram[(e - 1) * CAP:e * CAP, :].rearrange("(t p) d -> p t d", p=P),
                                 ys[:, (e - 1) % 2, :, :]).then_inc(ys_out[(e - 1) % 2], 16)
            if NX + 1 < NSETS:
                load_set(NX + 1)
            sp.wait_ge(ys_ready, NX)
            sp.dma_start(ys_dram[(NX - 1) * CAP:, :].rearrange("(t p) d -> p t d", p=P),
                         ys[:, (NX - 1) % 2, :, :]).then_inc(ys_out[(NX - 1) % 2], 16)
            with overflow(sp):
                with sp.Fori(0, NX) as e:
                    sp.wait_ge(o_sum, e * SHARED_BLOCKS + 1)
                    g, d = w_raw[:, 0, part_of(0)], w_raw[:, 0, part_of(1)]
                    sp.dma_start(g.rearrange("p (k n) -> p k n", k=KE),
                                 wgu[bass.ds(e, 1)].rearrange("a (k p) n -> p (a k) n", p=P)).then_inc(o_w, 16)
                    sp.dma_start(d.rearrange("p (f n) -> p f n", f=KF),
                                 wd[bass.ds(e, 1)].rearrange("a (f p) n -> p (a f) n", p=P)).then_inc(o_w, 16)
            for t in range(NT):
                sp.wait_ge(done, t + 1)
                sp.dma_start(out[t * P:(t + 1) * P, :], back[:, t, :]).then_inc(stored, 16)
            sp.wait_ge(stored, 16 * NT)

        @block.gpsimd
        def _(pool):
            pool.memset(zero[:, :], 0.0).then_inc(zeroed, 1)
            pool.memset(kbd[:, :, :, :, :].bitcast(FP32), 0.0).then_inc(init, 1)
            pool.memset(v_s[:, :, :, :, :], 0.0).then_inc(init, 1)
            pool.wait_ge(init, 2)
            pool.wait_ge(ld_c, 16 * 5)
            for b in range(B):
                for t in range(TT):
                    i = b * TT + t
                    pool.wait_ge(rope_in, i + 1)
                    if i >= TT:
                        pool.wait_ge(rope_sum, i - TT + 1)
                    qk = qkv[:, t, 0:HR * D].rearrange("p (h s d) -> p h s d", h=HR, s=2)
                    pool.tensor_tensor(rot_s[:, t, :, 0, :], qk[:, :, 1, :], sin_s[:, t, :, 0, :],
                                       ALU.mult).then_inc(rope_sin, 1)
                    pool.tensor_tensor(rot_s[:, t, :, 1, :], qk[:, :, 0, :], sin_s[:, t, :, 1, :],
                                       ALU.mult).then_inc(rope_sin, 1)
                    if b >= 2:
                        pool.wait_ge(pv_done, GB * (b - 1))
                    pool.tensor_copy(v_s[:, b % 2, t, :, 0:D],
                                     qkv[:, t, HR * D:].rearrange("p (h d) -> p h d", h=HKV)
                                     ).then_inc(v_ready, 1)

            def split_low(s, part):
                pool.wait_ge(w_high, 2 * s + part + 1)
                c = half_of(part, 1)
                pool.tensor_tensor(w_l[:, s % 2, c], w_raw[:, s % RAW, c],
                                   w_h[:, s % 2, c].bitcast(FP32), ALU.subtract).then_inc(w_low_pool, 1)

            for s in range(2):
                split_low(s, 0)
                split_low(s, 1)
            pool.wait_ge(slot_ready, 1)
            pool.wait_ge(zero_rows, 16 * NX * TT)
            for t in range(NT):
                pool.wait_ge(scaled, t + 1)
                pool.indirect_dma_start(xs_dram, bass.IndirectOffsetOnAxis(ap=slot_u[:, t:t + 1], axis=0),
                                        x1s[:, t % 2, :], None, bounds_check=NSLOT - 1,
                                        oob_is_err=False).then_inc(scattered[t % 2], 16)
            pool.wait_ge(misc_full, use_at[("kT", B - 1, 0)] + 1)
            pool.memset(back, 0.0).then_inc(back_zero, 1)
            for s in range(2, NSETS):
                split_low(s, 0)
                split_low(s, 1)
            pool.wait_ge(back_zero, 1)
            pool.wait_ge(ys_out[0], 16 * (NX // 2))
            pool.wait_ge(ys_out[1], 16 * (NX // 2))
            for t in range(NT):
                pool.indirect_dma_start(back[:, t, :], None, ys_dram,
                                        bass.IndirectOffsetOnAxis(ap=slot_u[:, t:t + 1], axis=0),
                                        bounds_check=NSLOT - 1, oob_is_err=False).then_inc(got[t], 16)

        @block.scalar
        def _(act):
            act.dma_start(bias_s[:, :], bqkv.broadcast_to((P, NQKV))).then_inc(ld_c, 16)
            act.dma_start(cos_s[:, :, :, :], cosq.rearrange("(t p) (h d) -> p t h d", p=P, h=HR)).then_inc(ld_c, 16)
            act.dma_start(sin_s[:, :, :, :, :],
                          sinq.rearrange("(t p) (h s d) -> p t h s d", p=P, h=HR, s=2)).then_inc(ld_c, 16)
            act.dma_start(cf_s[:, :], cf).then_inc(ld_c, 16)
            act.dma_start(masks_f, cb).then_inc(ld_c, 16)

            def high_parts(b, t):
                i = b * TT + t
                act.wait_ge(rope_sum, i + 1)
                if b:
                    act.wait_ge(misc_full, use_at[("kT", b - 1, 0)] + 1)
                act.activation(q4[:, t, :, 0:2, :], rot[:, t, 0:HQ, :].unsqueeze(2).broadcast_to((P, HQ, 2, D)),
                               ACT.Copy).then_inc(q_high, 1)
                act.activation(k4[:, t, :, :, 0, :], rot[:, t, HQ:, :].unsqueeze(2).broadcast_to((P, HKV, 4, D)),
                               ACT.Copy).then_inc(q_high, 1)

            def exps(p):
                b, u = divmod(p, PAIRS)
                act.wait_ge(max_ready, 2 * p + 2)
                if p >= 2:
                    act.wait_ge(pt_full, 2 * (p - 1))
                s = SCORES[p % 2]
                for j in range(2):
                    h = 2 * u + j
                    for t, src, dst in ((1, bank[s][:, j * L:(j + 1) * L], probs[:, p % 2, j, 0:L]),
                                        (0, bank[s + 1][:, j * P:(j + 1) * P], probs[:, p % 2, j, L:L + P])):
                        act.activation(dst, src, ACT.Exp, bias=negmax[:, b, t, h:h + 1],
                                       accum_out=denom[:, b, t, h:h + 1]).then_inc(exp_ready, 1)

            def serve(use):
                kind, b, i = use
                at = use_at[use]
                if kind == "qT" and i % 2 == 0:
                    act.wait_ge(misc_full, at + 1)
                    act.activation(q4T[:, b % 2, 0:4, (i // 2) * P:(i // 2 + 1) * P],
                                   bank[MISC][:, :].rearrange("p (a q) -> p a q", a=4),
                                   ACT.Copy).then_inc(qT_act, 1)
                    act.wait_ge(qT_act, b * 2 + i // 2 + 1)
                    act.sem_inc(misc_free, 1)
                elif kind == "kT":
                    act.wait_ge(misc_full, at + 1)
                    for j in range(2):
                        act.activation(kbd[64 * j:64 * j + 64, b % 2, :, j, :].rearrange("p h (t k) -> p t h k", t=TT),
                                       bank[MISC][64 * j:64 * j + 64, :].rearrange("p (t h k) -> p t h k", t=TT, h=HKV),
                                       ACT.Copy).then_inc(kT_ready, 1)
                    act.wait_ge(kT_ready, 2 * b + 2)
                    act.sem_inc(misc_free, 1)
                elif kind == "onT":
                    act.wait_ge(misc_full, at + 1)
                    act.activation(onT_s[:, :, :, :].rearrange("p t k q -> p (t k q)"), bank[MISC][:, :],
                                   ACT.Copy).then_inc(onT_ready, 1)
                    act.wait_ge(onT_ready, b + 1)
                    act.sem_inc(misc_free, 1)

            def o_evac(g):
                act.wait_ge(pv_done, g + 1)
                if g >= GB:
                    act.wait_ge(misc_full, use_at[("otr", g // GB - 1, 1)] + 1)
                act.activation(oT_s[:, g % GB, :], bank[OT][:, 0:L], ACT.Copy).then_inc(o_ev, 1)

            for t in range(TT):
                high_parts(0, t)
            for use in first_uses:
                serve(use)
            exps(0)
            for p in range(NP):
                b, u = divmod(p, PAIRS)
                if p + 1 < NP:
                    exps(p + 1)
                act.wait_ge(pt_full, 2 * p + 2)
                if p >= 4:
                    act.wait_ge(pv_done, p // 2 - 1)
                act.activation(probsT[:, (p // 2) % 2, 2 * (p % 2) + 1, :], bank[PT[1]][:, 0:L + P],
                               ACT.Copy).then_inc(pt_ev[1], 1)
                if p % 2 == 0 and p:
                    o_evac(p // 2 - 1)
                for use in slot_uses[p]:
                    serve(use)
                if b + 1 < B and u in (1, 2):
                    high_parts(b + 1, u - 1)
            o_evac(NG - 1)
            for use in slot_uses[NP]:
                serve(use)

            def split_high(s, part):
                act.wait_ge(raw_in[s % RAW], 16 * (3 if s == 0 else 2) if s < RAW
                            else 16 * (2 * (s // RAW) + (3 if s % RAW == 0 else 2)))
                if s >= 2 and part == 0:
                    act.wait_ge(gu_full, (last_block(s - 2) + 1) * KF)
                elif s >= 2:
                    act.wait_ge(y_full, last_block(s - 2) + 1)
                c = part_of(part)
                act.activation(w_h[:, s % 2, c], w_raw[:, s % RAW, c], ACT.Copy).then_inc(w_high, 1)

            for s in range(2):
                split_high(s, 0)
                split_high(s, 1)
            act.wait_ge(var_ready, 1)
            act.activation(std[:, :], mv[:, :, 1], ACT.Sqrt).then_inc(std_ready, 1)
            for c in range(NT // 2):
                act.wait_ge(x1T_full, c + 1)
                act.activation(x1T_h[:, :, c * 2 * P:(c + 1) * 2 * P],
                               bank[c % 2][:, :].rearrange("p (k q) -> p k q", k=KE),
                               ACT.Copy).then_inc(x1T_high, 1)
            act.wait_ge(top_ready, 1)
            act.activation(score[:, :], top[:, :], ACT.Sigmoid).then_inc(score_ready, 1)

            def silu(n, f):
                i = n * KF + f
                act.wait_ge(gu_full, i + 1)
                if i >= 2:
                    act.wait_ge(h_ready, i - 1)
                act.activation(gate[:, i % 2, :], bank[4 + i % 4][:, 0:CAP], ACT.Silu).then_inc(gate_ready, 1)

            def h_split(n, f):
                i = n * KF + f
                act.wait_ge(h_ready, i + 1)
                if n >= 2:
                    act.wait_ge(y_full, n - 1)
                act.activation(hT_h[:, n % 2, f, :], hT[:, i % 2, :], ACT.Copy).then_inc(h_high, 1)

            def xs_high(e):
                act.wait_ge(xsT_full, e + 1)
                if e >= 2:
                    act.wait_ge(gu_full, (SHARED_BLOCKS + e - 1) * KF)
                act.activation(xsT_h[:, e % 2, :, :], bank[2 + e % 2][:, :].rearrange("p (k q) -> p k q", k=KE),
                               ACT.Copy).then_inc(xsT_high, 1)

            def ys_copy(e):
                n = SHARED_BLOCKS + e
                act.wait_ge(y_full, n + 1)
                if e >= 2:
                    act.wait_ge(ys_out[e % 2], 16 * (e // 2))
                act.activation(ys[:, e % 2, :, :].rearrange("p t d -> p (t d)"), bank[n % 2][:, :],
                               ACT.Copy).then_inc(ys_ready, 1)

            for n in range(NB):
                for f in range(KF):
                    silu(n, f)
                    if f:
                        h_split(n, f - 1)
                    if f == 1 and n > SHARED_BLOCKS:
                        e = n - 1 - SHARED_BLOCKS
                        ys_copy(e)
                    if f == 3 and n + 1 >= SHARED_BLOCKS and n + 1 < NB:
                        xs_high(n + 1 - SHARED_BLOCKS)
                    if f % 2 == 0 and n >= SHARED_BLOCKS and set_of(n) + 1 < NSETS:
                        split_high(set_of(n) + 1, f // 2)
                h_split(n, KF - 1)
            ys_copy(NX - 1)
            with overflow(act):
                with act.Fori(0, NX * SHARED_BLOCKS) as i:
                    for f in range(KF):
                        act.wait_ge(o_gu, i * KF + f + 1)
                        act.wait_ge(o_h, i * KF + f + 1)
                        act.activation(gate[:, 0, :], bank[4][:, 0:CAP], ACT.Silu).then_inc(o_gate, 1)
            act.wait_ge(var2, 1)
            act.activation(std[:, :], mv[:, :, 1], ACT.Sqrt).then_inc(std2, 1)

        @block.vector
        def _(dve):
            links = [0]

            def link(ins):
                links[0] += 1
                ins.then_inc(dve_link, 1)
                dve.wait_ge(dve_link, links[0])

            def low_parts(b, t):
                i = b * TT + t
                dve.wait_ge(q_high, 2 * i + 2)
                dve.tensor_tensor(q4[:, t, :, 2:4, :], rot[:, t, 0:HQ, :].unsqueeze(2).broadcast_to((P, HQ, 2, D)),
                                  q4[:, t, :, 0:2, :].bitcast(FP32), ALU.subtract).then_inc(q_low, 1)
                dve.tensor_tensor(k4[:, t, :, :, 1, :], rot[:, t, HQ:, :].unsqueeze(2).broadcast_to((P, HKV, 4, D)),
                                  k4[:, t, :, :, 0, :].bitcast(FP32), ALU.subtract).then_inc(q_low, 1)

            def serve(use):
                kind, b, i = use
                at = use_at[use]
                if kind == "proj":
                    n = b * TT + i
                    dve.wait_ge(misc_full, at + 1)
                    if b:
                        dve.wait_ge(v_ready, n - TT + 1)
                    dve.tensor_tensor(qkv[:, i, :], bank[MISC][:, 0:NQKV], bias_s[:, :],
                                      ALU.add).then_inc(rope_in, 1)
                    dve.wait_ge(rope_in, n + 1)
                    dve.sem_inc(misc_free, 1)
                    link(dve.tensor_tensor(rot_c[:, i, :, :], qkv[:, i, 0:HR * D].rearrange("p (h d) -> p h d", h=HR),
                                           cos_s[:, i, :, :], ALU.mult))
                    dve.wait_ge(rope_sin, 2 * n + 2)
                    if b:
                        dve.wait_ge(q_low, 2 * (n - TT) + 2)
                        dve.wait_ge(q_high, 2 * (n - TT) + 2)
                    dve.tensor_tensor(rot[:, i, :, :], rot_c[:, i, :, :],
                                      rot_s[:, i, :, :, :].rearrange("p h s d -> p h (s d)"),
                                      ALU.add).then_inc(rope_sum, 1)
                elif kind == "qT" and i % 2 == 1:
                    dve.wait_ge(misc_full, at + 1)
                    dve.tensor_copy(q4T[:, b % 2, 4:8, (i // 2) * P:(i // 2 + 1) * P],
                                    bank[MISC][:, :].rearrange("p (a q) -> p a q", a=4)).then_inc(qT_dve, 1)
                    dve.wait_ge(qT_dve, b * 2 + i // 2 + 1)
                    dve.sem_inc(misc_free, 1)
                elif kind == "otr":
                    dve.wait_ge(misc_full, at + 1)
                    if i == 0:
                        if b:
                            dve.wait_ge(misc_full, use_at[("onT", b - 1, 0)] + 1)
                        link(dve.reciprocal(rdenom[:, :, :], denom[:, b, :, :]))
                    dve.tensor_tensor(on[:, i, :, :],
                                      bank[MISC][:, :].rearrange("p (h d) -> p h d", d=2 * D)[:, :, 0:D],
                                      rdenom[:, i, :].unsqueeze(2).broadcast_to((P, HQ, D)),
                                      ALU.mult).then_inc(on_ready, 1)
                    dve.wait_ge(on_ready, b * TT + i + 1)
                    dve.sem_inc(misc_free, 1)
                elif kind == "wo":
                    dve.wait_ge(misc_full, at + 1)
                    dve.wait_ge(ld_r, 32)
                    dve.tensor_tensor(r1[:, b * TT:(b + 1) * TT, :],
                                      bank[MISC][:, :].rearrange("p (t e) -> p t e", t=TT),
                                      r1[:, b * TT:(b + 1) * TT, :], ALU.add).then_inc(r1_ready, 1)
                    dve.wait_ge(r1_ready, b + 1)
                    dve.sem_inc(misc_free, 1)
                    for t in range(b * TT, (b + 1) * TT):
                        last = dve.bn_stats(stats[:, t, :], r1[:, t, :])
                    link(last)
                    for t in range(b * TT, (b + 1) * TT):
                        last = dve.bn_aggr(mv[:, t, :], stats[:, t, :])
                    link(last)

            def maxes(p):
                b, u = divmod(p, PAIRS)
                dve.wait_ge(scores_full, p + 1)
                s = SCORES[p % 2]
                dve.reduce_max(negmax[:, b, 1, 2 * u:2 * u + 2], bank[s][:, :].rearrange("p (h k) -> p h k", h=2),
                               AX.X, negate=True).then_inc(max_ready, 1)
                dve.reduce_max(negmax[:, b, 0, 2 * u:2 * u + 2],
                               bank[s + 1][:, 0:2 * P].rearrange("p (h k) -> p h k", h=2),
                               AX.X, negate=True).then_inc(max_ready, 1)

            dve.wait_ge(ld_c, 16 * 5)
            dve.tensor_copy(cb_s[:, :], masks_f).then_inc(masks_ready, 1)
            for use in first_uses:
                serve(use)
                if use[0] == "proj":
                    low_parts(0, use[2])
            maxes(0)
            maxes(1)
            for p in range(NP):
                b, u = divmod(p, PAIRS)
                dve.wait_ge(pt_full, 2 * p + 1)
                if p >= 4:
                    dve.wait_ge(pv_done, p // 2 - 1)
                dve.tensor_copy(probsT[:, (p // 2) % 2, 2 * (p % 2), :],
                                bank[PT[0]][:, 0:L + P]).then_inc(pt_ev[0], 1)
                if p + 2 < NP:
                    maxes(p + 2)
                for use in slot_uses[p]:
                    serve(use)
                if b + 1 < B and u in (1, 2):
                    low_parts(b + 1, u - 1)
            for use in slot_uses[NP]:
                serve(use)
            dve.tensor_scalar(mv[:, :, 1], mv[:, :, 1], EPS, None, ALU.add).then_inc(var_ready, 1)
            dve.wait_ge(std_ready, 1)
            link(dve.reciprocal(rstd[:, :], std[:, :]))
            for t in range(NT):
                dve.tensor_scalar(r1[:, t, :], r1[:, t, :], mv[:, t, 0:1], rstd[:, t:t + 1],
                                  ALU.subtract, ALU.mult).then_inc(x1_ready, 1)
            link(dve.tensor_copy(rw_r[:, :, 0, :], rw_s[:, :, :]))
            dve.tensor_tensor(rw_r[:, :, 1, :], rw_s[:, :, :], rw_r[:, :, 0, :].bitcast(FP32),
                              ALU.subtract).then_inc(rw_ready, 1)
            for c in range(NT // 2):
                dve.wait_ge(x1T_high, c + 1)
                cols = slice(c * 2 * P, (c + 1) * 2 * P)
                dve.tensor_tensor(x1T_l[:, :, cols], bank[c % 2][:, :].rearrange("p (k q) -> p k q", k=KE),
                                  x1T_h[:, :, cols].bitcast(FP32), ALU.subtract).then_inc(x1T_low, 1)

            def split_low(s, part):
                dve.wait_ge(w_high, 2 * s + part + 1)
                c = half_of(part, 0)
                dve.tensor_tensor(w_l[:, s % 2, c], w_raw[:, s % RAW, c],
                                  w_h[:, s % 2, c].bitcast(FP32), ALU.subtract).then_inc(w_low_dve, 1)

            split_low(0, 0)
            split_low(0, 1)
            dve.wait_ge(logits_full, 1)
            parts = bank[2][:, 0:NT * 2 * NX].rearrange("p (t s e) -> p t s e", t=NT, s=2)
            link(dve.tensor_copy(pick[:, :, :], parts[:, :, 0, :]))
            link(dve.tensor_tensor(lg[:, :, :], pick[:, :, :], parts[:, :, 1, :], ALU.add))
            dve.reduce_max(top[:, :], lg[:, :, :], AX.X).then_inc(top_ready, 1)
            dve.wait_ge(top_ready, 1)
            link(dve.tensor_tensor(pick[:, :, :], lg[:, :, :], top[:, :].unsqueeze(2).broadcast_to((P, NT, NX)),
                                   ALU.is_lt))
            link(dve.scalar_tensor_tensor(out=place[:, :, :], in0=pick[:, :, :], scalar=float(NX),
                                          in1=expert_no.unsqueeze(1).broadcast_to((P, NT, NX)),
                                          op0=ALU.mult, op1=ALU.add))
            link(dve.tensor_reduce(first[:, :], place[:, :, :], AX.X, ALU.min))
            fb = first[:, :].unsqueeze(2).broadcast_to((P, NT, NX))
            xb = expert_no.unsqueeze(1).broadcast_to((P, NT, NX))
            dve.tensor_tensor(onehot[:, :, :], xb, fb, ALU.is_equal)
            dve.tensor_tensor(onehot_b[:, :, :], xb, fb, ALU.is_equal).then_inc(onehot_ready, 1)
            link(dve.tensor_scalar(base[:, :], expert_no, float(CAP), None, ALU.mult))
            dve.wait_ge(onehot_ready, 1)
            dve.wait_ge(rank_full, 1)
            link(dve.tensor_tensor(place[:, :, :], bank[3][:, 0:NT * NX].rearrange("p (t e) -> p t e", t=NT),
                                   base[:, :].unsqueeze(1).broadcast_to((P, NT, NX)), ALU.add))
            link(dve.tensor_tensor(place[:, :, :], place[:, :, :], onehot[:, :, :], ALU.mult))
            link(dve.reduce_sum(slot_f[:, :], place[:, :, :], AX.X))
            link(dve.tensor_scalar(base[:, :], expert_no, float(CAP), float(CAP), ALU.mult, ALU.add))
            link(dve.tensor_tensor(place[:, :, :], onehot[:, :, :],
                                   base[:, :].unsqueeze(1).broadcast_to((P, NT, NX)), ALU.mult))
            link(dve.reduce_sum(over[:, :], place[:, :, :], AX.X))
            link(dve.tensor_tensor(over[:, :], slot_f[:, :], over[:, :], ALU.is_ge))
            dve.tensor_copy(over_b[:, :], over[:, :]).then_inc(over_ready, 1)
            link(dve.scalar_tensor_tensor(out=slot_f[:, :], in0=over[:, :], scalar=float(NSLOT),
                                          in1=slot_f[:, :], op0=ALU.mult, op1=ALU.add))
            dve.tensor_copy(slot_u[:, :], slot_f[:, :]).then_inc(slot_ready, 1)
            dve.tensor_tensor(over_mask[:, :, :], onehot[:, :, :],
                              over[:, :].unsqueeze(2).broadcast_to((P, NT, NX)), ALU.mult)
            dve.wait_ge(over_full, 1)
            link(dve.reduce_sum(n_over_f[:, :], bank[3][:, NT * NX:NT * NX + NT], AX.X))
            dve.tensor_copy(n_over[:, :], n_over_f[:, :]).then_inc(n_over_ready, 1)
            dve.wait_ge(score_ready, 1)

            def scale_rows(t):
                if t >= 2:
                    dve.wait_ge(scattered[t % 2], 16 * (t // 2))
                dve.tensor_scalar(x1s[:, t % 2, :], r1[:, t, :], score[:, t:t + 1], None,
                                  ALU.mult).then_inc(scaled, 1)

            def h_product(n, f):
                i = n * KF + f
                dve.wait_ge(gate_ready, i + 1)
                if i >= 2:
                    dve.wait_ge(h_high, i - 1)
                    dve.wait_ge(h_low, i - 1)
                dve.tensor_tensor(hT[:, i % 2, :], bank[4 + i % 4][:, CAP:2 * CAP], gate[:, i % 2, :],
                                  ALU.mult).then_inc(h_ready, 1)

            def h_rest(n, f):
                i = n * KF + f
                dve.wait_ge(h_high, i + 1)
                dve.tensor_tensor(hT_l[:, n % 2, f, :], hT[:, i % 2, :], hT_h[:, n % 2, f, :].bitcast(FP32),
                                  ALU.subtract).then_inc(h_low, 1)

            def xs_low(e):
                dve.wait_ge(xsT_high, e + 1)
                dve.tensor_tensor(xsT_l[:, e % 2, :, :], bank[2 + e % 2][:, :].rearrange("p (k q) -> p k q", k=KE),
                                  xsT_h[:, e % 2, :, :].bitcast(FP32), ALU.subtract).then_inc(xsT_low, 1)

            rows = 0
            for n in range(NB):
                for f in range(KF):
                    h_product(n, f)
                    if f:
                        h_rest(n, f - 1)
                    if f == 1 and 1 <= n <= SHARED_BLOCKS:
                        dve.wait_ge(y_full, n)
                        dve.tensor_tensor(y_sh[:, (n - 1) * TT:n * TT, :],
                                          bank[(n - 1) % 2][:, :].rearrange("p (t e) -> p t e", t=TT),
                                          r1[:, (n - 1) * TT:n * TT, :], ALU.add).then_inc(y_sh_ready, 1)
                    if f == 3 and n + 1 >= SHARED_BLOCKS and n + 1 < NB:
                        xs_low(n + 1 - SHARED_BLOCKS)
                    if rows < NT:
                        scale_rows(rows)
                        rows += 1
                    if f % 2 == 0 and (n == 0 or n >= SHARED_BLOCKS) and set_of(n) + 1 < NSETS:
                        split_low(set_of(n) + 1, f // 2)
                h_rest(n, KF - 1)
            with overflow(dve):
                dve.sem_inc(o_h, 1)
                dve.sem_inc(o_sum, 1)
                with dve.Fori(0, NX) as e:
                    with dve.Fori(0, SHARED_BLOCKS) as c:
                        i = e * SHARED_BLOCKS + c
                        for t in range(TT):
                            dve.tensor_scalar(xs[:, 0, t, :],
                                              r1[:, bass.ds(c * TT + t, 1), :].rearrange("p a e -> p (a e)"),
                                              score[:, bass.ds(c * TT + t, 1)], None, ALU.mult
                                              ).then_inc(o_rows, 1)
                        dve.wait_ge(o_xT_full, i + 1)
                        dve.tensor_copy(xsT_o, bank[2][:, :].rearrange("p (k c) -> p k c", k=KE)
                                        ).then_inc(o_xT, 1)
                        for f in range(KF):
                            dve.wait_ge(o_gate, i * KF + f + 1)
                            dve.tensor_tensor(hT_o[:, f, :], bank[4][:, CAP:2 * CAP], gate[:, 0, :],
                                              ALU.mult).then_inc(o_h, 1)
                        dve.wait_ge(o_y, i + 1)
                        for t in range(TT):
                            rows = y_sh[:, bass.ds(c * TT + t, 1), :].rearrange("p a e -> p (a e)")
                            last = dve.scalar_tensor_tensor(
                                out=rows, in0=bank[0][:, t * E:(t + 1) * E],
                                scalar=over_mask[:, bass.ds(c * TT + t, 1), bass.ds(e, 1)].rearrange("p a b -> p (a b)"),
                                in1=rows, op0=ALU.mult, op1=ALU.add)
                        last.then_inc(o_sum, 1)
                        dve.wait_ge(o_sum, i + 2)
            for t in range(NT):
                dve.wait_ge(got[t], 16)
                link(dve.tensor_tensor(y_sh[:, t, :], y_sh[:, t, :], back[:, t, :], ALU.add))
                link(dve.bn_stats(stats[:, t, :], y_sh[:, t, :]))
                link(dve.bn_aggr(mv[:, t, :], stats[:, t, :]))
            dve.tensor_scalar(mv[:, :, 1], mv[:, :, 1], EPS, None, ALU.add).then_inc(var2, 1)
            dve.wait_ge(std2, 1)
            link(dve.reciprocal(rstd[:, :], std[:, :]))
            for t in range(NT):
                dve.tensor_scalar(back[:, t, :], y_sh[:, t, :], mv[:, t, 0:1], rstd[:, t:t + 1],
                                  ALU.subtract, ALU.mult).then_inc(done, 1)

        @block.tensor
        def _(pe):
            def scores(p):
                b, u = divmod(p, PAIRS)
                kv = u // (PAIRS // HKV)
                s = SCORES[p % 2]
                if p >= 2:
                    pe.wait_ge(exp_ready, 4 * (p - 1))
                if u == 0:
                    pe.wait_ge(qT_act, 2 * b + 2)
                    pe.wait_ge(qT_dve, 2 * b + 2)
                    pe.wait_ge(kT_ready, 2 * b + 2)
                pe.matmul(bank[s][:, :], q4T[:, b % 2, u, P:L],
                          kbd[:, b % 2, kv, :, :].rearrange("p h k -> p (h k)"), start=True, stop=False)
                pe.matmul(bank[s][:, :].rearrange("p (h k) -> p h k", h=2)[:, :, P:L], ident_b, mask2,
                          start=False, stop=True)
                pe.matmul(bank[s + 1][:, 0:2 * P].rearrange("p (h k) -> p h k", h=2), q4T[:, b % 2, u, 0:P],
                          kbd[:, b % 2, kv, :, 0:P], start=True, stop=False)
                pe.matmul(bank[s + 1][:, 0:2 * P].rearrange("p (h k) -> p h k", h=2), ident_b, mask2,
                          start=False, stop=True).then_inc(scores_full, 1)

            def transpose_probs(p, j):
                pe.wait_ge(exp_ready, 4 * p + 2 * j + 2)
                if p:
                    pe.wait_ge(pt_ev[j], p)
                pr = probs[:, p % 2, j, :]
                for dst, src in ((0, L), (P, 0), (2 * P, P)):
                    last = pe.transpose(bank[PT[j]][:, dst:dst + P], pr[:, src:src + P], ident)
                last.then_inc(pt_full, 1)

            def weigh_values(g):
                b = g // GB
                kv = (g % GB) // (GB // HKV)
                pe.wait_ge(pt_ev[0], 2 * g + 2)
                pe.wait_ge(pt_ev[1], 2 * g + 2)
                if g:
                    pe.wait_ge(o_ev, g)
                if g % GB == 0:
                    pe.wait_ge(v_ready, TT * (b + 1))
                for k, src, dst in ((0, 0, 0), (1, L, P)):
                    for j in range(4):
                        last = pe.matmul(bank[OT][32 * j:32 * j + 32, dst:L], v_s[:, b % 2, k, kv, :],
                                         probsT[:, g % 2, j, src:src + L - dst], start=(k == 0), stop=(k == 1))
                last.then_inc(pv_done, 1)

            def misc(use):
                kind, b, i = use
                at = use_at[use]
                if at:
                    pe.wait_ge(misc_free, at)
                bk = bank[MISC]
                if kind == "proj":
                    for k in range(KE):
                        last = pe.matmul(bk[:, 0:NQKV], xT_s[:, k, (b * TT + i) * P:(b * TT + i + 1) * P],
                                         wqkv_s[:, k, :], start=(k == 0), stop=(k == KE - 1))
                elif kind == "qT":
                    t, half = divmod(i, 2)
                    pe.wait_ge(q_low, 2 * (b * TT + t) + 2)
                    for a in range(4):
                        h = 2 * (4 * half + a)
                        last = pe.transpose(bk[:, a * P:(a + 1) * P],
                                            q4[:, t, h:h + 2, :, :].bitcast(FP32).rearrange("p h s d -> p (h s d)"),
                                            ident)
                elif kind == "kT":
                    for t in range(TT):
                        for h in range(HKV):
                            at2 = t * HKV + h
                            last = pe.transpose(bk[:, at2 * P:(at2 + 1) * P],
                                                k4[:, t, h, :, :, :].bitcast(FP32).rearrange("p a s d -> p (a s d)"),
                                                ident)
                elif kind == "otr":
                    pe.wait_ge(o_ev, GB * (b + 1))
                    for g in range(GB):
                        last = pe.transpose(bk[:, g * P:(g + 1) * P], oT_s[:, g, i * P:(i + 1) * P], ident)
                elif kind == "onT":
                    pe.wait_ge(on_ready, TT * (b + 1))
                    for t in range(TT):
                        for k in range(KE):
                            at2 = t * KE + k
                            last = pe.transpose(bk[:, at2 * P:(at2 + 1) * P],
                                                on[:, t, 8 * k:8 * k + 8, :].rearrange("p h d -> p (h d)"), ident)
                else:
                    pe.wait_ge(onT_ready, b + 1)
                    for t in range(TT):
                        for k in range(KE):
                            last = pe.matmul(bk[:, t * E:(t + 1) * E], onT_s[:, t, k, :], wo_s[:, k, :],
                                             start=(k == 0), stop=(k == KE - 1))
                last.then_inc(misc_full, 1)

            pe.wait_ge(ld_x, 32)
            for use in first_uses:
                if use[0] == "qT":
                    pe.wait_ge(ld_c, 16 * 5)
                misc(use)
            pe.wait_ge(init, 2)
            pe.wait_ge(masks_ready, 1)
            scores(0)
            scores(1)
            pe.wait_ge(ld_w, 32)
            for p in range(NP):
                transpose_probs(p, 0)
                if p + 2 < NP:
                    scores(p + 2)
                transpose_probs(p, 1)
                if p % 2 == 0 and p:
                    weigh_values(p // 2 - 1)
                for use in slot_uses[p]:
                    misc(use)
            weigh_values(NG - 1)
            for use in slot_uses[NP]:
                misc(use)

            for c in range(NT // 2):
                pe.wait_ge(x1_ready, 2 * c + 2)
                if c >= 2:
                    pe.wait_ge(x1T_low, c - 1)
                for k in range(KE):
                    for t in range(2):
                        last = pe.transpose(bank[c % 2][:, (2 * k + t) * P:(2 * k + t + 1) * P],
                                            r1[:, 2 * c + t, k * P:(k + 1) * P], ident)
                last.then_inc(x1T_full, 1)
            pe.wait_ge(rw_ready, 1)
            pe.wait_ge(x1T_low, NT // 2)
            for t in range(NT):
                o = bank[2][:, t * 2 * NX:(t + 1) * 2 * NX]
                for k in range(KE):
                    pe.matmul(o, x1T_h[:, k, t * P:(t + 1) * P], rw_r[:, k, :, :].rearrange("p s e -> p (s e)"),
                              start=(k == 0), stop=False)
                for k in range(KE):
                    last = pe.matmul(o[:, 0:NX], x1T_l[:, k, t * P:(t + 1) * P], rw_r[:, k, 0, :],
                                     start=False, stop=(k == KE - 1))
            last.then_inc(logits_full, 1)

            def products(n):
                if n < SHARED_BLOCKS:
                    c = slice(n * CAP, (n + 1) * CAP)
                    return [(x1T_h[:, k, c], x1T_l[:, k, c]) for k in range(KE)]
                e = n - SHARED_BLOCKS
                return [(xsT_h[:, e % 2, k, :], xsT_l[:, e % 2, k, :]) for k in range(KE)]

            def gate_up(n, f):
                i = n * KF + f
                par = set_of(n) % 2
                if f == 0:
                    pe.wait_ge(w_low_dve, 2 * set_of(n) + 1)
                    pe.wait_ge(w_low_pool, 2 * set_of(n) + 1)
                    if n >= SHARED_BLOCKS:
                        pe.wait_ge(xsT_low, n - SHARED_BLOCKS + 1)
                if i >= 4:
                    pe.wait_ge(h_ready, i - 3)
                xt = products(n)
                for up in range(2):
                    o = bank[4 + i % 4][:, up * CAP:(up + 1) * CAP]
                    for k in range(KE):
                        pe.matmul(o, gu(par, True, f, k, up), xt[k][0], start=(k == 0), stop=False)
                        pe.matmul(o, gu(par, True, f, k, up), xt[k][1], start=False, stop=False)
                        last = pe.matmul(o, gu(par, False, f, k, up), xt[k][0], start=False, stop=(k == KE - 1))
                last.then_inc(gu_full, 1)

            def down_rows(n):
                par = set_of(n) % 2
                pe.wait_ge(h_low, (n + 1) * KF)
                pe.wait_ge(w_low_dve, 2 * set_of(n) + 2)
                pe.wait_ge(w_low_pool, 2 * set_of(n) + 2)
                if n >= 2:
                    if n - 2 < SHARED_BLOCKS:
                        pe.wait_ge(y_sh_ready, n - 1)
                    else:
                        pe.wait_ge(ys_ready, n - 1 - SHARED_BLOCKS)
                for t in range(TT):
                    o = bank[n % 2][:, t * E:(t + 1) * E]
                    c = slice(t * P, (t + 1) * P)
                    for f in range(KF):
                        pe.matmul(o, hT_h[:, n % 2, f, c], down(par, True, f), start=(f == 0), stop=False)
                        pe.matmul(o, hT_h[:, n % 2, f, c], down(par, False, f), start=False, stop=False)
                        last = pe.matmul(o, hT_l[:, n % 2, f, c], down(par, True, f), start=False,
                                         stop=(f == KF - 1))
                last.then_inc(y_full, 1)

            def rows_T(e):
                pe.wait_ge(xs_in[e % 2], 16 * (e // 2 + 1))
                if e >= 2:
                    pe.wait_ge(xsT_low, e - 1)
                for k in range(KE):
                    for t in range(TT):
                        last = pe.transpose(bank[2 + e % 2][:, k * CAP + t * P:k * CAP + (t + 1) * P],
                                            xs[:, e % 2, t, k * P:(k + 1) * P], ident)
                last.then_inc(xsT_full, 1)

            for n in range(NB):
                for f in range(KF):
                    gate_up(n, f)
                    if n == 0 and f == 0:
                        pe.wait_ge(onehot_ready, 1)
                        o = bank[3][:, 0:NT * NX].rearrange("p (t e) -> p t e", t=NT)
                        pe.matmul(o, earlier, onehot_b[:, :, :], start=True, stop=False)
                        for s in range(1, NT):
                            last = pe.matmul(o[:, s:NT, :], ones_b, onehot_b[:, 0:NT - s, :], start=False,
                                             stop=(s == NT - 1))
                        last.then_inc(rank_full, 1)
                    if n == 0 and f == 1:
                        pe.wait_ge(over_ready, 1)
                        pe.matmul(bank[3][:, NT * NX:NT * NX + NT], ones_b, over_b[:, :], start=True,
                                  stop=True).then_inc(over_full, 1)
                    if f == 0 and n:
                        down_rows(n - 1)
                    if f == 2 and n + 1 >= SHARED_BLOCKS and n + 1 < NB:
                        rows_T(n + 1 - SHARED_BLOCKS)
            down_rows(NB - 1)
            with overflow(pe):
                with pe.Fori(0, NX) as e, pe.Fori(0, SHARED_BLOCKS) as c:
                    i = e * SHARED_BLOCKS + c
                    pe.wait_ge(o_rows, i * TT + TT)
                    for k in range(KE):
                        for t in range(TT):
                            last = pe.transpose(bank[2][:, k * CAP + t * P:k * CAP + (t + 1) * P],
                                                xs[:, 0, t, k * P:(k + 1) * P], ident)
                    last.then_inc(o_xT_full, 1)
                    pe.wait_ge(o_xT, i + 1)
                    pe.wait_ge(o_w, e * 32 + 32)
                    g, d = w_raw[:, 0, part_of(0)], w_raw[:, 0, part_of(1)]
                    g, d = g.rearrange("p (k n) -> p k n", k=KE), d.rearrange("p (f n) -> p f n", f=KF)
                    for f in range(KF):
                        pe.wait_ge(o_h, i * KF + f + 1)
                        for up in range(2):
                            for k in range(KE):
                                n = up * F + f * P
                                last = pe.matmul(bank[4][:, up * CAP:(up + 1) * CAP], g[:, k, n:n + P],
                                                 xsT_o[:, k, :], start=(k == 0), stop=(k == KE - 1))
                        last.then_inc(o_gu, 1)
                    pe.wait_ge(o_h, i * KF + KF + 1)
                    for t in range(TT):
                        for f in range(KF):
                            last = pe.matmul(bank[0][:, t * E:(t + 1) * E], hT_o[:, f, t * P:(t + 1) * P],
                                             d[:, f, :], start=(f == 0), stop=(f == KF - 1))
                    last.then_inc(o_y, 1)


def constants():
    half = np.arange(HALF, dtype=np.float32) / np.float32(HALF)
    inv = (np.float32(THETA) ** (-half)).astype(np.float32)
    ang = np.arange(L, dtype=np.float32)[:, None] * inv[None, :]
    cos, sin = np.cos(ang).astype(np.float32), np.sin(ang).astype(np.float32)
    scale = np.where(np.arange(HR) < HQ, np.float32(D ** -0.5), np.float32(1.0)).astype(np.float32)
    cosq = np.concatenate([cos, cos], 1)[:, None, :] * scale[None, :, None]
    sinq = np.concatenate([-sin, sin], 1)[:, None, :] * scale[None, :, None]
    eye = np.eye(P, dtype=np.float32)
    cf = np.concatenate([eye, np.tile(np.arange(NX, dtype=np.float32), (P, 1))], 1)
    k, q = np.arange(P)[None, :], np.arange(P)[:, None]
    mask = np.where(k > q, np.float32(MASKED), np.float32(0))
    earlier = (q < k).astype(np.float32)
    cb = np.concatenate([eye, mask, mask, earlier, np.ones((P, P), np.float32)], 1)
    return cosq.reshape(L, HR * D), sinq.reshape(L, HR * D), cf, cb


def kernel(**inputs):
    import concourse.bacc as bacc
    from concourse.bass_utils import run_bass_kernel_spmd

    a = {n: np.asarray(v) for n, v in inputs.items()}
    x = a["L0_attn_x"].reshape(T, E)
    cosq, sinq, cf, cb = constants()
    arrays = {
        "x": x,
        "xT": x.T,
        "wqkvT": np.concatenate([a["L0_attn_wq"], a["L0_attn_wk"], a["L0_attn_wv"]], 0).T,
        "bqkv": np.concatenate([a["L0_attn_bq"], a["L0_attn_bk"], a["L0_attn_bv"]])[None, :],
        "woT": a["L0_attn_wo"].T,
        "rwT": a["L0_ffn_router_w"].T,
        "wgu": a["L0_ffn_gate_up_proj"],
        "wd": a["L0_ffn_down_proj"],
        "swg": a["L0_ffn_shared_gate_w"],
        "swu": a["L0_ffn_shared_up_w"],
        "swd": a["L0_ffn_shared_down_w"],
        "cosq": cosq, "sinq": sinq, "cf": cf, "cb": cb,
    }
    arrays = {n: np.ascontiguousarray(v) for n, v in arrays.items()}
    nc = bacc.Bacc("TRN2", target_bir_lowering=False, num_devices=1)
    args = [nc.dram_tensor(n, v.shape, mybir.dt.from_np(v.dtype), kind="ExternalInput").ap()
            for n, v in arrays.items()]
    out = nc.dram_tensor("out", (T, E), FP32, kind="ExternalOutput").ap()
    program(nc, *args, out)
    r = run_bass_kernel_spmd(nc, [arrays], core_ids=[0])
    return r.results[0]["out"].reshape(B, L, E)
```

```python
import numpy as np
import concourse.bass as bass
from concourse import mybir
from contextlib import ExitStack

FP32 = mybir.dt.float32
FP32R = mybir.dt.float32r
BF16 = mybir.dt.bfloat16
U32 = mybir.dt.uint32
I32 = mybir.dt.int32
ALU = mybir.AluOpType
ACT = mybir.ActivationFunctionType
AX = mybir.AxisListType

P = 128
B, L, E = 4, 256, 256
T = B * L
NT = T // P
KE = E // P
HQ, HKV, D = 16, 2, 16
HALF = D // 2
HR = HQ + HKV
NQKV = (HQ + 2 * HKV) * D
NX, F = 8, 512
KF = F // P
TT = L // P
PAIRS = HQ // 2
NP = B * PAIRS
NG = NP // 2
GB = HQ // 4
CAP = 256
NSLOT = NX * CAP
THETA = 10000.0
EPS = 1e-5
MASKED = -1.0e30
WSET = KE * 2 * F + KF * E
NSETS = NX + 2
CHUNKS = T // CAP
SH1 = CHUNKS // 2
NB = CHUNKS + NX
SH2 = SH1 + NX
RAW = 3
RING = 3
EARLY = 2
QUARTER = WSET // 4


def misc_uses():
    slots = [[] for _ in range(NP + 1)]
    for b in range(B):
        at = PAIRS * b
        if b + 1 < B:
            slots[at] += [("proj", b + 1, 0)]
            slots[at + 1] += [("proj", b + 1, 1)]
            slots[at + 3] += [("qT", b + 1, 0)]
            slots[at + 4] += [("qT", b + 1, 1), ("qT", b + 1, 2)]
            slots[at + 5] += [("qT", b + 1, 3), ("kT", b + 1, 0)]
        if b:
            slots[at + 1] += [("otr", b - 1, 0)]
            slots[at + 2] += [("otr", b - 1, 1)]
            slots[at + 3] += [("onT", b - 1, 0)]
            slots[at + 6] += [("wo", b - 1, 0)]
    first = [("proj", 0, 0), ("proj", 0, 1)] + [("qT", 0, i) for i in range(4)] + [("kT", 0, 0)]
    slots[NP] = [("otr", B - 1, 0), ("otr", B - 1, 1), ("onT", B - 1, 0), ("wo", B - 1, 0)]
    order = first + [u for s in slots for u in s]
    return first, slots, {u: i for i, u in enumerate(order)}


def set_of(block):
    return min(max(block - SH1 + 1, 0), NSETS - 1)


def chunk_of(block):
    return block if block < SH1 else block - NX if block >= SH2 else None


def last_block(s):
    return SH1 - 1 + s


def part_of(part):
    return slice(0, KE * 2 * F) if part == 0 else slice(KE * 2 * F, WSET)


def quarter(q, half=None):
    if half is None:
        return slice(q * QUARTER, (q + 1) * QUARTER)
    return slice(q * QUARTER + half * QUARTER // 2, q * QUARTER + (half + 1) * QUARTER // 2)


def split_steps():
    steps = {}
    for s in range(EARLY, NSETS):
        free = 0 if s < RING else last_block(s - RING) + 1
        for q in range(4):
            steps.setdefault(divmod(free * KF + 1 + q, KF), []).append((s, q))
    return steps


def raw_loaded(s):
    return 16 * sum(3 if r in (0, NSETS - 1) else 2 for r in range(s % RAW, s + 1, RAW))


def split_count(s, q):
    return 4 * (s - EARLY) + q + 1


def program(nc, x, xT, wqkvT, bqkv, woT, rwT, wgu, wd, swg, swu, swd, cosq, sinq, cf, cb, out):
    first_uses, slot_uses, use_at = misc_uses()
    split_at = split_steps()
    xs_dram = nc.dram_tensor("xs_dram", (NSLOT, E), FP32).ap()
    ys_dram = nc.dram_tensor("ys_dram", (NSLOT, E), FP32).ap()

    ctx = ExitStack()
    with ctx:
        def sb(name, shape, dt=FP32):
            return ctx.enter_context(nc.sbuf_tensor(name, shape, dt))

        def sem(name):
            return ctx.enter_context(nc.semaphore(name))

        cf_s = sb("cf_s", [P, P + NX])
        cb_s = sb("cb_s", [P, 5 * P], BF16)
        ident = cf_s[:, 0:P]
        expert_no = cf_s[:, P:P + NX]
        ident_b = cb_s[:, 0:P]
        mask2 = cb_s[:, P:3 * P].rearrange("p (a k) -> p a k", a=2)
        earlier = cb_s[:, 3 * P:4 * P]
        ones_b = cb_s[:, 4 * P:5 * P]
        r1 = sb("r1", [P, NT, E])
        rw_s = sb("rw_s", [P, KE, NX])
        rw_r = sb("rw_r", [P, KE, 2, NX], FP32R)

        stats = sb("stats", [P, NT, 6])
        mv = sb("mv", [P, NT, 2])
        std = sb("std", [P, NT])
        rstd = sb("rstd", [P, NT])
        lg = sb("lg", [P, NT, NX])
        top = sb("top", [P, NT])
        pick = sb("pick", [P, NT, NX])
        first = sb("first", [P, NT])
        onehot = sb("onehot", [P, NT, NX])
        onehot_b = sb("onehot_b", [P, NT, NX], BF16)
        score = sb("score", [P, NT])
        place = sb("place", [P, NT, NX])
        slot_f = sb("slot_f", [P, NT])
        over = sb("over", [P, NT])
        over_b = sb("over_b", [P, NT], BF16)
        over_mask = sb("over_mask", [P, NT, NX])
        n_over_f = sb("n_over_f", [P, 1])
        n_over = sb("n_over", [P, 1], I32)
        slot_u = sb("slot_u", [P, NT], U32)
        base = sb("base", [P, NX])
        zero = sb("zero", [P, E])

        w_raw = sb("w_raw", [P, RAW, WSET])
        w_h = [sb(f"w_h{i}", [P, WSET], FP32R) for i in range(EARLY)]
        w_l = [sb(f"w_l{i}", [P, WSET], FP32R) for i in range(EARLY)]

        attention = ExitStack()

        def early(name, shape, dt=FP32):
            return attention.enter_context(nc.sbuf_tensor(name, shape, dt))

        xT_s = early("xT_s", [P, KE, T])
        wqkv_s = early("wqkv_s", [P, KE, NQKV])
        bias_s = early("bias_s", [P, NQKV])
        wo_s = early("wo_s", [P, KE, E])
        cos_s = early("cos_s", [P, TT, HR, D])
        sin_s = early("sin_s", [P, TT, HR, 2, HALF])
        qkv = early("qkv", [P, TT, NQKV])
        rot_c = early("rot_c", [P, TT, HR, D])
        rot_s = early("rot_s", [P, TT, HR, 2, HALF])
        rot = early("rot", [P, TT, HR, D])
        q4 = early("q4", [P, TT, HQ, 4, D], FP32R)
        k4 = early("k4", [P, TT, HKV, 4, 2, D], FP32R)
        q4T = early("q4T", [P, 2, PAIRS, L], FP32R)
        kbd = early("kbd", [P, 2, HKV, 2, L], FP32R)
        v_s = early("v_s", [P, 2, TT, HKV, 2 * D])
        negmax = early("negmax", [P, B, TT, HQ])
        denom = early("denom", [P, B, TT, HQ])
        rdenom = early("rdenom", [P, TT, HQ])
        probs = early("probs", [P, 2, 2, L + P])
        probsT = early("probsT", [P, 2, 4, L + P])
        oT_s = early("oT_s", [P, GB, L])
        on = early("on", [P, TT, HQ, D])
        onT_s = early("onT_s", [P, TT, KE, P])

        attention.close()

        x1T_h = sb("x1T_h", [P, KE, T], FP32R)
        x1T_l = sb("x1T_l", [P, KE, T], FP32R)
        x1s = sb("x1s", [P, NT, E])
        w_h += [sb(f"w_h{i}", [P, WSET], FP32R) for i in range(EARLY, RING)]
        w_l += [sb(f"w_l{i}", [P, WSET], FP32R) for i in range(EARLY, RING)]
        xs = sb("xs", [P, 2, TT, E])
        ys = sb("ys", [P, 2, TT, E])
        xsT_h = sb("xsT_h", [P, 2, KE, CAP], FP32R)
        xsT_l = sb("xsT_l", [P, 2, KE, CAP], FP32R)
        gate = sb("gate", [P, 2, CAP])
        hT = sb("hT", [P, 2, CAP])
        hT_h = sb("hT_h", [P, 2, KF, CAP], FP32R)
        hT_l = sb("hT_l", [P, 2, KF, CAP], FP32R)
        y_sh = sb("y_sh", [P, NT, E])
        back = sb("back", [P, NT, E])

        bank = [ctx.enter_context(nc.psum_tensor(f"bank{i}", [P, 512], FP32)) for i in range(8)]
        SCORES, PT, OT, MISC = [0, 2], [4, 5], 6, 7

        masks_f = probs[:, :, :, :].rearrange("p a j q -> p (a j q)")[:, 0:5 * P]
        spare = w_raw[:, 1, :]
        xsT_o = spare[:, 0:KE * CAP].rearrange("p (k c) -> p k c", k=KE)
        hT_o = spare[:, KE * CAP:(KE + KF) * CAP].rearrange("p (f c) -> p f c", f=KF)

        ld_c, ld_x, ld_w, ld_r = sem("ld_consts"), sem("ld_x"), sem("ld_wo"), sem("ld_tok")
        raw_in = [sem(f"raw_in{i}") for i in range(RAW)]
        init, masks_ready = sem("init"), sem("masks_ready")
        misc_full, misc_free = sem("misc_full"), sem("misc_free")
        rope_in, rope_sin, rope_sum, q_high, q_low = (
            sem("rope_in"), sem("rope_sin"), sem("rope_sum"), sem("q_high"), sem("q_low"))
        v_ready = sem("v_ready")
        qT_act, qT_dve = sem("qT_act"), sem("qT_dve")
        kT_ready = sem("kT_ready")
        scores_full, max_ready, exp_ready = sem("scores_full"), sem("max_ready"), sem("exp_ready")
        pt_full, pt_ev = sem("pt_full"), [sem("pt_ev0"), sem("pt_ev1")]
        pv_done, o_ev = sem("pv_done"), sem("o_ev")
        on_ready, onT_ready, r1_ready = sem("on_ready"), sem("onT_ready"), sem("r1_ready")
        dve_link = sem("dve_link")
        var_ready, std_ready, x1_ready = sem("var_ready"), sem("std_ready"), sem("x1_ready")
        x1T_full, x1T_high, x1T_low = sem("x1T_full"), sem("x1T_high"), sem("x1T_low")
        rw_ready = sem("rw_ready")
        logits_full, onehot_ready, rank_full = sem("logits_full"), sem("onehot_ready"), sem("rank_full")
        top_ready, score_ready, slot_ready = sem("top_ready"), sem("score_ready"), sem("slot_ready")
        scaled, zeroed = sem("scaled"), sem("zeroed")
        zero_rows = sem("zero_rows")
        scattered = sem("scattered")
        w_high, w_low_dve, w_low_pool = sem("w_high"), sem("w_low_dve"), sem("w_low_pool")
        early_high, early_low = sem("early_high"), sem("early_low")
        xs_in = [sem("xs_in0"), sem("xs_in1")]
        xsT_full, xsT_high, xsT_low = sem("xsT_full"), sem("xsT_high"), sem("xsT_low")
        gu_full, gate_ready, h_ready, h_high, h_low = (
            sem("gu_full"), sem("gate_ready"), sem("h_ready"), sem("h_high"), sem("h_low"))
        y_full, y_sh_ready, ys_ready = sem("y_full"), sem("y_sh_ready"), sem("ys_ready")
        ys_out = [sem("ys_out0"), sem("ys_out1")]
        got = [sem(f"got{t}") for t in range(NT)]
        var2, std2, done = sem("var2"), sem("std2"), sem("done")
        stored = sem("stored")
        over_ready, over_full, n_over_ready = sem("over_ready"), sem("over_full"), sem("n_over_ready")
        back_zero = sem("back_zero")
        o_w, o_rows, o_xT_full, o_xT, o_gu, o_gate, o_h, o_y, o_sum, o_link = (
            sem("o_weights"), sem("o_rows"), sem("o_xT_full"), sem("o_xT"), sem("o_gate_up"),
            sem("o_gate"), sem("o_h"), sem("o_y"), sem("o_sum"), sem("o_link"))
        block = ctx.enter_context(nc.Block())

        def gu(par, high, f, k, up):
            w = (w_h if high else w_l)[par][:, 0:KE * 2 * F].rearrange("p (k n) -> p k n", k=KE)
            return w[:, k, up * F + f * P:up * F + (f + 1) * P]

        def down(par, high, f):
            w = (w_h if high else w_l)[par][:, KE * 2 * F:].rearrange("p (f n) -> p f n", f=KF)
            return w[:, f, :]

        def overflow(eng):
            eng.wait_ge(n_over_ready, 1)
            return eng.If(eng.value_load(n_over[0:1, 0:1], min_val=0, max_val=T) > 0)

        @block.sync
        def _(sp):
            sp.dma_start(wqkv_s[:, :, :], wqkvT.rearrange("(k p) n -> p k n", p=P)).then_inc(ld_x, 16)
            xTv = xT.rearrange("(k p) t -> p k t", p=P)
            sp.dma_start(xT_s[:, :, 0:L], xTv[:, :, 0:L]).then_inc(ld_x, 16)
            sp.dma_start(xT_s[:, :, L:T], xTv[:, :, L:T]).then_inc(ld_w, 16)
            sp.dma_start(wo_s[:, :, :], woT.rearrange("(k p) n -> p k n", p=P)).then_inc(ld_w, 16)
            sp.dma_start(r1[:, :, :], x.rearrange("(t p) e -> p t e", p=P)).then_inc(ld_r, 16)
            sp.dma_start(rw_s[:, :, :], rwT.rearrange("(k p) n -> p k n", p=P)).then_inc(ld_r, 16)
            sp.wait_ge(zeroed, 1)
            for e in range(NX):
                for t in range(TT):
                    at = (e * TT + t) * P
                    sp.dma_start(xs_dram[at:at + P, :], zero[:, :]).then_inc(zero_rows, 16)

            def load_set(s):
                if s >= RAW:
                    if s - RAW < EARLY:
                        sp.wait_ge(early_low, 4 * (s - RAW) + 4)
                    else:
                        sp.wait_ge(w_low_dve, split_count(s - RAW, 3))
                        sp.wait_ge(w_low_pool, split_count(s - RAW, 3))
                r = w_raw[:, s % RAW, :]
                g, d = r[:, 0:KE * 2 * F].rearrange("p (k n) -> p k n", k=KE), r[:, KE * 2 * F:]
                if s in (0, NSETS - 1):
                    sp.dma_start(g[:, :, 0:F], swg.rearrange("(k p) n -> p k n", p=P)).then_inc(raw_in[s % RAW], 16)
                    sp.dma_start(g[:, :, F:], swu.rearrange("(k p) n -> p k n", p=P)).then_inc(raw_in[s % RAW], 16)
                    src = swd
                else:
                    sp.dma_start(g, wgu[s - 1].rearrange("(k p) n -> p k n", p=P)).then_inc(raw_in[s % RAW], 16)
                    src = wd[s - 1]
                sp.dma_start(d.rearrange("p (f n) -> p f n", f=KF),
                             src.rearrange("(f p) n -> p f n", p=P)).then_inc(raw_in[s % RAW], 16)

            for s in range(RAW):
                load_set(s)
            for s in range(RAW, 4):
                load_set(s)

            def store_rows(e):
                sp.wait_ge(ys_ready, e + 1)
                sp.dma_start(ys_dram[e * CAP:(e + 1) * CAP, :].rearrange("(t p) d -> p t d", p=P),
                             ys[:, e % 2, :, :]).then_inc(ys_out[e % 2], 16)

            sp.wait_ge(scattered, 16 * NT)
            for e in range(NX):
                if e >= 2:
                    sp.wait_ge(xsT_full, e - 1)
                sp.dma_start(xs[:, e % 2, :, :],
                             xs_dram[e * CAP:(e + 1) * CAP, :].rearrange("(t p) d -> p t d", p=P)
                             ).then_inc(xs_in[e % 2], 16)
                if e + 4 < NSETS:
                    load_set(e + 4)
                if e >= 2:
                    store_rows(e - 2)
            store_rows(NX - 2)
            store_rows(NX - 1)
            with overflow(sp):
                with sp.Fori(0, NX) as e:
                    sp.wait_ge(o_sum, e * CHUNKS + 1)
                    g, d = w_raw[:, 0, part_of(0)], w_raw[:, 0, part_of(1)]
                    sp.dma_start(g.rearrange("p (k n) -> p k n", k=KE),
                                 wgu[bass.ds(e, 1)].rearrange("a (k p) n -> p (a k) n", p=P)).then_inc(o_w, 16)
                    sp.dma_start(d.rearrange("p (f n) -> p f n", f=KF),
                                 wd[bass.ds(e, 1)].rearrange("a (f p) n -> p (a f) n", p=P)).then_inc(o_w, 16)
            for t in range(NT):
                sp.wait_ge(done, t + 1)
                sp.dma_start(out[t * P:(t + 1) * P, :], back[:, t, :]).then_inc(stored, 16)
            sp.wait_ge(stored, 16 * NT)

        @block.gpsimd
        def _(pool):
            pool.memset(zero[:, :], 0.0).then_inc(zeroed, 1)
            pool.memset(kbd[:, :, :, :, :].bitcast(FP32), 0.0).then_inc(init, 1)
            pool.memset(v_s[:, :, :, :, :], 0.0).then_inc(init, 1)
            pool.wait_ge(init, 2)
            pool.wait_ge(ld_c, 16 * 5)

            def split_early(s, q):
                c = quarter(q)
                pool.wait_ge(raw_in[s], raw_loaded(s))
                pool.tensor_scalar(w_h[s][:, c], w_raw[:, s, c], 1.0, None, ALU.mult).then_inc(early_high, 1)
                pool.wait_ge(early_high, 4 * s + q + 1)
                pool.tensor_tensor(w_l[s][:, c], w_raw[:, s, c], w_h[s][:, c].bitcast(FP32),
                                   ALU.subtract).then_inc(early_low, 1)

            early_quarters = [(s, q) for s in range(EARLY) for q in range(4)]
            for b in range(B):
                for t in range(TT):
                    i = b * TT + t
                    pool.wait_ge(rope_in, i + 1)
                    if i >= TT:
                        pool.wait_ge(rope_sum, i - TT + 1)
                    qk = qkv[:, t, 0:HR * D].rearrange("p (h s d) -> p h s d", h=HR, s=2)
                    pool.tensor_tensor(rot_s[:, t, :, 0, :], qk[:, :, 1, :], sin_s[:, t, :, 0, :],
                                       ALU.mult).then_inc(rope_sin, 1)
                    pool.tensor_tensor(rot_s[:, t, :, 1, :], qk[:, :, 0, :], sin_s[:, t, :, 1, :],
                                       ALU.mult).then_inc(rope_sin, 1)
                    if b >= 2:
                        pool.wait_ge(pv_done, GB * (b - 1))
                    pool.tensor_copy(v_s[:, b % 2, t, :, 0:D],
                                     qkv[:, t, HR * D:].rearrange("p (h d) -> p h d", h=HKV)
                                     ).then_inc(v_ready, 1)
                if b:
                    for s, q in early_quarters[3 * (b - 1):3 * b]:
                        split_early(s, q)

            def split_low(s, q):
                pool.wait_ge(w_high, split_count(s, q))
                c = quarter(q, 1)
                pool.tensor_tensor(w_l[s % RING][:, c], w_raw[:, s % RAW, c],
                                   w_h[s % RING][:, c].bitcast(FP32), ALU.subtract).then_inc(w_low_pool, 1)

            pool.wait_ge(slot_ready, 1)
            pool.wait_ge(zero_rows, 16 * NX * TT)
            for t in range(NT):
                pool.wait_ge(scaled, t + 1)
                pool.indirect_dma_start(xs_dram, bass.IndirectOffsetOnAxis(ap=slot_u[:, t:t + 1], axis=0),
                                        x1s[:, t, :], None, bounds_check=NSLOT - 1,
                                        oob_is_err=False).then_inc(scattered, 16)
            pool.wait_ge(x1T_full, 1)
            pool.memset(back[:, :, :], 0.0).then_inc(back_zero, 1)
            for s in range(EARLY, NSETS):
                for q in range(4):
                    split_low(s, q)
            pool.wait_ge(back_zero, 1)
            pool.wait_ge(ys_out[0], 16 * (NX // 2))
            pool.wait_ge(ys_out[1], 16 * (NX // 2))
            for t in range(NT):
                pool.indirect_dma_start(back[:, t, :], None, ys_dram,
                                        bass.IndirectOffsetOnAxis(ap=slot_u[:, t:t + 1], axis=0),
                                        bounds_check=NSLOT - 1, oob_is_err=False).then_inc(got[t], 16)

        @block.scalar
        def _(act):
            act.dma_start(bias_s[:, :], bqkv.broadcast_to((P, NQKV))).then_inc(ld_c, 16)
            act.dma_start(cos_s[:, :, :, :], cosq.rearrange("(t p) (h d) -> p t h d", p=P, h=HR)).then_inc(ld_c, 16)
            act.dma_start(sin_s[:, :, :, :, :],
                          sinq.rearrange("(t p) (h s d) -> p t h s d", p=P, h=HR, s=2)).then_inc(ld_c, 16)
            act.dma_start(cf_s[:, :], cf).then_inc(ld_c, 16)
            act.dma_start(masks_f, cb).then_inc(ld_c, 16)

            def high_parts(b, t):
                i = b * TT + t
                act.wait_ge(rope_sum, i + 1)
                if b:
                    act.wait_ge(misc_full, use_at[("kT", b - 1, 0)] + 1)
                act.activation(q4[:, t, :, 0:2, :], rot[:, t, 0:HQ, :].unsqueeze(2).broadcast_to((P, HQ, 2, D)),
                               ACT.Copy).then_inc(q_high, 1)
                act.activation(k4[:, t, :, :, 0, :], rot[:, t, HQ:, :].unsqueeze(2).broadcast_to((P, HKV, 4, D)),
                               ACT.Copy).then_inc(q_high, 1)

            def exps(p):
                b, u = divmod(p, PAIRS)
                act.wait_ge(max_ready, 2 * p + 2)
                if p >= 2:
                    act.wait_ge(pt_full, 2 * (p - 1))
                s = SCORES[p % 2]
                for j in range(2):
                    h = 2 * u + j
                    for t, src, dst in ((1, bank[s][:, j * L:(j + 1) * L], probs[:, p % 2, j, 0:L]),
                                        (0, bank[s + 1][:, j * P:(j + 1) * P], probs[:, p % 2, j, L:L + P])):
                        act.activation(dst, src, ACT.Exp, bias=negmax[:, b, t, h:h + 1],
                                       accum_out=denom[:, b, t, h:h + 1]).then_inc(exp_ready, 1)

            def serve(use):
                kind, b, i = use
                at = use_at[use]
                if kind == "qT" and i % 2 == 0:
                    act.wait_ge(misc_full, at + 1)
                    act.activation(q4T[:, b % 2, 0:4, (i // 2) * P:(i // 2 + 1) * P],
                                   bank[MISC][:, :].rearrange("p (a q) -> p a q", a=4),
                                   ACT.Copy).then_inc(qT_act, 1)
                    act.wait_ge(qT_act, b * 2 + i // 2 + 1)
                    act.sem_inc(misc_free, 1)
                elif kind == "kT":
                    act.wait_ge(misc_full, at + 1)
                    for j in range(2):
                        act.activation(kbd[64 * j:64 * j + 64, b % 2, :, j, :].rearrange("p h (t k) -> p t h k", t=TT),
                                       bank[MISC][64 * j:64 * j + 64, :].rearrange("p (t h k) -> p t h k", t=TT, h=HKV),
                                       ACT.Copy).then_inc(kT_ready, 1)
                    act.wait_ge(kT_ready, 2 * b + 2)
                    act.sem_inc(misc_free, 1)
                elif kind == "onT":
                    act.wait_ge(misc_full, at + 1)
                    act.activation(onT_s[:, :, :, :].rearrange("p t k q -> p (t k q)"), bank[MISC][:, :],
                                   ACT.Copy).then_inc(onT_ready, 1)
                    act.wait_ge(onT_ready, b + 1)
                    act.sem_inc(misc_free, 1)

            def o_evac(g):
                act.wait_ge(pv_done, g + 1)
                if g >= GB:
                    act.wait_ge(misc_full, use_at[("otr", g // GB - 1, 1)] + 1)
                act.activation(oT_s[:, g % GB, :], bank[OT][:, 0:L], ACT.Copy).then_inc(o_ev, 1)

            for t in range(TT):
                high_parts(0, t)
            for use in first_uses:
                serve(use)
            exps(0)
            for p in range(NP):
                b, u = divmod(p, PAIRS)
                if p + 1 < NP:
                    exps(p + 1)
                act.wait_ge(pt_full, 2 * p + 2)
                if p >= 4:
                    act.wait_ge(pv_done, p // 2 - 1)
                act.activation(probsT[:, (p // 2) % 2, 2 * (p % 2) + 1, :], bank[PT[1]][:, 0:L + P],
                               ACT.Copy).then_inc(pt_ev[1], 1)
                if p % 2 == 0 and p:
                    o_evac(p // 2 - 1)
                for use in slot_uses[p]:
                    serve(use)
                if b + 1 < B and u in (1, 2):
                    high_parts(b + 1, u - 1)
            o_evac(NG - 1)
            for use in slot_uses[NP]:
                serve(use)

            def split_high(s, q):
                act.wait_ge(raw_in[s % RAW], raw_loaded(s))
                if s >= RING:
                    act.wait_ge(y_full, last_block(s - RING) + 1)
                c = quarter(q)
                act.activation(w_h[s % RING][:, c], w_raw[:, s % RAW, c], ACT.Copy).then_inc(w_high, 1)

            act.wait_ge(var_ready, 1)
            act.activation(std[:, :], mv[:, :, 1], ACT.Sqrt).then_inc(std_ready, 1)
            for c in range(NT // 2):
                act.wait_ge(x1T_full, c + 1)
                act.activation(x1T_h[:, :, c * 2 * P:(c + 1) * 2 * P],
                               bank[c % 2][:, :].rearrange("p (k q) -> p k q", k=KE),
                               ACT.Copy).then_inc(x1T_high, 1)
            act.wait_ge(top_ready, 1)
            act.activation(score[:, :], top[:, :], ACT.Sigmoid).then_inc(score_ready, 1)

            def silu(n, f):
                i = n * KF + f
                act.wait_ge(gu_full, i + 1)
                if i >= 2:
                    act.wait_ge(h_ready, i - 1)
                act.activation(gate[:, i % 2, :], bank[4 + i % 4][:, 0:CAP], ACT.Silu).then_inc(gate_ready, 1)

            def h_split(n, f):
                i = n * KF + f
                act.wait_ge(h_ready, i + 1)
                if n >= 2:
                    act.wait_ge(y_full, n - 1)
                act.activation(hT_h[:, n % 2, f, :], hT[:, i % 2, :], ACT.Copy).then_inc(h_high, 1)

            def xs_high(e):
                act.wait_ge(xsT_full, e + 1)
                if e >= 2:
                    act.wait_ge(gu_full, (SH1 + e - 1) * KF)
                act.activation(xsT_h[:, e % 2, :, :], bank[2 + e % 2][:, :].rearrange("p (k q) -> p k q", k=KE),
                               ACT.Copy).then_inc(xsT_high, 1)

            def ys_copy(e):
                n = SH1 + e
                act.wait_ge(y_full, n + 1)
                if e >= 2:
                    act.wait_ge(ys_out[e % 2], 16 * (e // 2))
                act.activation(ys[:, e % 2, :, :].rearrange("p t d -> p (t d)"), bank[n % 2][:, :],
                               ACT.Copy).then_inc(ys_ready, 1)

            for n in range(NB):
                for f in range(KF):
                    if f == 2 and SH1 <= n + 1 < SH2:
                        xs_high(n + 1 - SH1)
                    silu(n, f)
                    if f:
                        h_split(n, f - 1)
                    if f == 1 and SH1 <= n - 1 < SH2:
                        ys_copy(n - 1 - SH1)
                    for s, q in split_at.get((n, f), []):
                        split_high(s, q)
                h_split(n, KF - 1)
            with overflow(act):
                with act.Fori(0, NX * CHUNKS) as i:
                    for f in range(KF):
                        act.wait_ge(o_gu, i * KF + f + 1)
                        act.wait_ge(o_h, i * KF + f + 1)
                        act.activation(gate[:, 0, :], bank[4][:, 0:CAP], ACT.Silu).then_inc(o_gate, 1)
            act.wait_ge(var2, 1)
            act.activation(std[:, :], mv[:, :, 1], ACT.Sqrt).then_inc(std2, 1)

        @block.vector
        def _(dve):
            links = [0]

            def link(ins):
                links[0] += 1
                ins.then_inc(dve_link, 1)
                dve.wait_ge(dve_link, links[0])

            def low_parts(b, t):
                i = b * TT + t
                dve.wait_ge(q_high, 2 * i + 2)
                dve.tensor_tensor(q4[:, t, :, 2:4, :], rot[:, t, 0:HQ, :].unsqueeze(2).broadcast_to((P, HQ, 2, D)),
                                  q4[:, t, :, 0:2, :].bitcast(FP32), ALU.subtract).then_inc(q_low, 1)
                dve.tensor_tensor(k4[:, t, :, :, 1, :], rot[:, t, HQ:, :].unsqueeze(2).broadcast_to((P, HKV, 4, D)),
                                  k4[:, t, :, :, 0, :].bitcast(FP32), ALU.subtract).then_inc(q_low, 1)

            def serve(use):
                kind, b, i = use
                at = use_at[use]
                if kind == "proj":
                    n = b * TT + i
                    dve.wait_ge(misc_full, at + 1)
                    if b:
                        dve.wait_ge(v_ready, n - TT + 1)
                    dve.tensor_tensor(qkv[:, i, :], bank[MISC][:, 0:NQKV], bias_s[:, :],
                                      ALU.add).then_inc(rope_in, 1)
                    dve.wait_ge(rope_in, n + 1)
                    dve.sem_inc(misc_free, 1)
                    link(dve.tensor_tensor(rot_c[:, i, :, :], qkv[:, i, 0:HR * D].rearrange("p (h d) -> p h d", h=HR),
                                           cos_s[:, i, :, :], ALU.mult))
                    dve.wait_ge(rope_sin, 2 * n + 2)
                    if b:
                        dve.wait_ge(q_low, 2 * (n - TT) + 2)
                        dve.wait_ge(q_high, 2 * (n - TT) + 2)
                    dve.tensor_tensor(rot[:, i, :, :], rot_c[:, i, :, :],
                                      rot_s[:, i, :, :, :].rearrange("p h s d -> p h (s d)"),
                                      ALU.add).then_inc(rope_sum, 1)
                elif kind == "qT" and i % 2 == 1:
                    dve.wait_ge(misc_full, at + 1)
                    dve.tensor_copy(q4T[:, b % 2, 4:8, (i // 2) * P:(i // 2 + 1) * P],
                                    bank[MISC][:, :].rearrange("p (a q) -> p a q", a=4)).then_inc(qT_dve, 1)
                    dve.wait_ge(qT_dve, b * 2 + i // 2 + 1)
                    dve.sem_inc(misc_free, 1)
                elif kind == "otr":
                    dve.wait_ge(misc_full, at + 1)
                    if i == 0:
                        if b:
                            dve.wait_ge(misc_full, use_at[("onT", b - 1, 0)] + 1)
                        link(dve.reciprocal(rdenom[:, :, :], denom[:, b, :, :]))
                    dve.tensor_tensor(on[:, i, :, :],
                                      bank[MISC][:, :].rearrange("p (h d) -> p h d", d=2 * D)[:, :, 0:D],
                                      rdenom[:, i, :].unsqueeze(2).broadcast_to((P, HQ, D)),
                                      ALU.mult).then_inc(on_ready, 1)
                    dve.wait_ge(on_ready, b * TT + i + 1)
                    dve.sem_inc(misc_free, 1)
                elif kind == "wo":
                    dve.wait_ge(misc_full, at + 1)
                    dve.wait_ge(ld_r, 32)
                    dve.tensor_tensor(r1[:, b * TT:(b + 1) * TT, :],
                                      bank[MISC][:, :].rearrange("p (t e) -> p t e", t=TT),
                                      r1[:, b * TT:(b + 1) * TT, :], ALU.add).then_inc(r1_ready, 1)
                    dve.wait_ge(r1_ready, b + 1)
                    dve.sem_inc(misc_free, 1)
                    for t in range(b * TT, (b + 1) * TT):
                        last = dve.bn_stats(stats[:, t, :], r1[:, t, :])
                    link(last)
                    for t in range(b * TT, (b + 1) * TT):
                        last = dve.bn_aggr(mv[:, t, :], stats[:, t, :])
                    link(last)

            def maxes(p):
                b, u = divmod(p, PAIRS)
                dve.wait_ge(scores_full, p + 1)
                s = SCORES[p % 2]
                dve.reduce_max(negmax[:, b, 1, 2 * u:2 * u + 2], bank[s][:, :].rearrange("p (h k) -> p h k", h=2),
                               AX.X, negate=True).then_inc(max_ready, 1)
                dve.reduce_max(negmax[:, b, 0, 2 * u:2 * u + 2],
                               bank[s + 1][:, 0:2 * P].rearrange("p (h k) -> p h k", h=2),
                               AX.X, negate=True).then_inc(max_ready, 1)

            dve.wait_ge(ld_c, 16 * 5)
            dve.tensor_copy(cb_s[:, :], masks_f).then_inc(masks_ready, 1)
            for use in first_uses:
                serve(use)
                if use[0] == "proj":
                    low_parts(0, use[2])
            maxes(0)
            maxes(1)
            for p in range(NP):
                b, u = divmod(p, PAIRS)
                dve.wait_ge(pt_full, 2 * p + 1)
                if p >= 4:
                    dve.wait_ge(pv_done, p // 2 - 1)
                dve.tensor_copy(probsT[:, (p // 2) % 2, 2 * (p % 2), :],
                                bank[PT[0]][:, 0:L + P]).then_inc(pt_ev[0], 1)
                if p + 2 < NP:
                    maxes(p + 2)
                for use in slot_uses[p]:
                    serve(use)
                if b + 1 < B and u in (1, 2):
                    low_parts(b + 1, u - 1)
            for use in slot_uses[NP]:
                serve(use)
            dve.tensor_scalar(mv[:, :, 1], mv[:, :, 1], EPS, None, ALU.add).then_inc(var_ready, 1)
            dve.wait_ge(std_ready, 1)
            link(dve.reciprocal(rstd[:, :], std[:, :]))
            for t in range(NT):
                dve.tensor_scalar(r1[:, t, :], r1[:, t, :], mv[:, t, 0:1], rstd[:, t:t + 1],
                                  ALU.subtract, ALU.mult).then_inc(x1_ready, 1)
            link(dve.tensor_copy(rw_r[:, :, 0, :], rw_s[:, :, :]))
            dve.tensor_tensor(rw_r[:, :, 1, :], rw_s[:, :, :], rw_r[:, :, 0, :].bitcast(FP32),
                              ALU.subtract).then_inc(rw_ready, 1)
            for c in range(NT // 2):
                dve.wait_ge(x1T_high, c + 1)
                cols = slice(c * 2 * P, (c + 1) * 2 * P)
                dve.tensor_tensor(x1T_l[:, :, cols], bank[c % 2][:, :].rearrange("p (k q) -> p k q", k=KE),
                                  x1T_h[:, :, cols].bitcast(FP32), ALU.subtract).then_inc(x1T_low, 1)

            def split_low(s, q):
                dve.wait_ge(w_high, split_count(s, q))
                c = quarter(q, 0)
                dve.tensor_tensor(w_l[s % RING][:, c], w_raw[:, s % RAW, c],
                                  w_h[s % RING][:, c].bitcast(FP32), ALU.subtract).then_inc(w_low_dve, 1)

            dve.wait_ge(logits_full, 1)
            parts = bank[2][:, 0:NT * 2 * NX].rearrange("p (t s e) -> p t s e", t=NT, s=2)
            link(dve.tensor_copy(pick[:, :, :], parts[:, :, 0, :]))
            link(dve.tensor_tensor(lg[:, :, :], pick[:, :, :], parts[:, :, 1, :], ALU.add))
            dve.reduce_max(top[:, :], lg[:, :, :], AX.X).then_inc(top_ready, 1)
            dve.wait_ge(top_ready, 1)
            link(dve.tensor_tensor(pick[:, :, :], lg[:, :, :], top[:, :].unsqueeze(2).broadcast_to((P, NT, NX)),
                                   ALU.is_lt))
            link(dve.scalar_tensor_tensor(out=place[:, :, :], in0=pick[:, :, :], scalar=float(NX),
                                          in1=expert_no.unsqueeze(1).broadcast_to((P, NT, NX)),
                                          op0=ALU.mult, op1=ALU.add))
            link(dve.tensor_reduce(first[:, :], place[:, :, :], AX.X, ALU.min))
            fb = first[:, :].unsqueeze(2).broadcast_to((P, NT, NX))
            xb = expert_no.unsqueeze(1).broadcast_to((P, NT, NX))
            dve.tensor_tensor(onehot[:, :, :], xb, fb, ALU.is_equal)
            dve.tensor_tensor(onehot_b[:, :, :], xb, fb, ALU.is_equal).then_inc(onehot_ready, 1)
            link(dve.tensor_scalar(base[:, :], expert_no, float(CAP), None, ALU.mult))
            dve.wait_ge(onehot_ready, 1)
            dve.wait_ge(rank_full, 1)
            link(dve.tensor_tensor(place[:, :, :], bank[3][:, 0:NT * NX].rearrange("p (t e) -> p t e", t=NT),
                                   base[:, :].unsqueeze(1).broadcast_to((P, NT, NX)), ALU.add))
            link(dve.tensor_tensor(place[:, :, :], place[:, :, :], onehot[:, :, :], ALU.mult))
            link(dve.reduce_sum(slot_f[:, :], place[:, :, :], AX.X))
            link(dve.tensor_scalar(base[:, :], expert_no, float(CAP), float(CAP), ALU.mult, ALU.add))
            link(dve.tensor_tensor(place[:, :, :], onehot[:, :, :],
                                   base[:, :].unsqueeze(1).broadcast_to((P, NT, NX)), ALU.mult))
            link(dve.reduce_sum(over[:, :], place[:, :, :], AX.X))
            link(dve.tensor_tensor(over[:, :], slot_f[:, :], over[:, :], ALU.is_ge))
            dve.tensor_copy(over_b[:, :], over[:, :]).then_inc(over_ready, 1)
            link(dve.scalar_tensor_tensor(out=slot_f[:, :], in0=over[:, :], scalar=float(NSLOT),
                                          in1=slot_f[:, :], op0=ALU.mult, op1=ALU.add))
            dve.tensor_copy(slot_u[:, :], slot_f[:, :]).then_inc(slot_ready, 1)
            dve.wait_ge(score_ready, 1)
            for t in range(NT):
                dve.tensor_scalar(x1s[:, t, :], r1[:, t, :], score[:, t:t + 1], None, ALU.mult).then_inc(scaled, 1)
            dve.tensor_tensor(over_mask[:, :, :], onehot[:, :, :],
                              over[:, :].unsqueeze(2).broadcast_to((P, NT, NX)), ALU.mult)
            dve.wait_ge(over_full, 1)
            link(dve.reduce_sum(n_over_f[:, :], bank[3][:, NT * NX:NT * NX + NT], AX.X))
            dve.tensor_copy(n_over[:, :], n_over_f[:, :]).then_inc(n_over_ready, 1)
            def h_product(n, f):
                i = n * KF + f
                dve.wait_ge(gate_ready, i + 1)
                if i >= 2:
                    dve.wait_ge(h_high, i - 1)
                    dve.wait_ge(h_low, i - 1)
                dve.tensor_tensor(hT[:, i % 2, :], bank[4 + i % 4][:, CAP:2 * CAP], gate[:, i % 2, :],
                                  ALU.mult).then_inc(h_ready, 1)

            def h_rest(n, f):
                i = n * KF + f
                dve.wait_ge(h_high, i + 1)
                dve.tensor_tensor(hT_l[:, n % 2, f, :], hT[:, i % 2, :], hT_h[:, n % 2, f, :].bitcast(FP32),
                                  ALU.subtract).then_inc(h_low, 1)

            def xs_low(e):
                dve.wait_ge(xsT_high, e + 1)
                dve.tensor_tensor(xsT_l[:, e % 2, :, :], bank[2 + e % 2][:, :].rearrange("p (k q) -> p k q", k=KE),
                                  xsT_h[:, e % 2, :, :].bitcast(FP32), ALU.subtract).then_inc(xsT_low, 1)

            def chunk(a, c):
                return a[:, c * TT:(c + 1) * TT, :]

            def add_shared(n):
                c = chunk_of(n)
                dve.wait_ge(y_full, n + 1)
                dve.tensor_tensor(chunk(y_sh, c), bank[n % 2][:, :].rearrange("p (t e) -> p t e", t=TT),
                                  chunk(y_sh if n == NB - 1 else r1, c), ALU.add).then_inc(y_sh_ready, 1)

            def add_routed(c):
                for t in range(c * TT, (c + 1) * TT):
                    dve.wait_ge(got[t], 16)
                    last = dve.tensor_tensor(y_sh[:, t, :], (r1 if c == CHUNKS - 1 else y_sh)[:, t, :],
                                             back[:, t, :], ALU.add)
                return last

            def moments(c, link=link):
                for t in range(c * TT, (c + 1) * TT):
                    last = dve.bn_stats(stats[:, t, :], y_sh[:, t, :])
                link(last)
                for t in range(c * TT, (c + 1) * TT):
                    last = dve.bn_aggr(mv[:, t, :], stats[:, t, :])
                return last

            for n in range(NB):
                for f in range(KF):
                    if f == 2 and SH1 <= n + 1 < SH2:
                        xs_low(n + 1 - SH1)
                    h_product(n, f)
                    if f:
                        h_rest(n, f - 1)
                    if f == 1 and n and chunk_of(n - 1) is not None:
                        add_shared(n - 1)
                    for s, q in split_at.get((n, f), []):
                        split_low(s, q)
                h_rest(n, KF - 1)
            for c in range(CHUNKS):
                if c == CHUNKS - 1:
                    link(add_routed(c))
                    add_shared(NB - 1)
                    dve.wait_ge(y_sh_ready, CHUNKS)
                else:
                    if c == CHUNKS - 2:
                        dve.wait_ge(y_sh_ready, CHUNKS - 1)
                    link(add_routed(c))
                last = moments(c)
            link(last)
            with overflow(dve):
                dve.sem_inc(o_h, 1)
                dve.sem_inc(o_sum, 1)
                with dve.Fori(0, NX) as e:
                    with dve.Fori(0, CHUNKS) as c:
                        i = e * CHUNKS + c
                        for t in range(TT):
                            dve.tensor_scalar(xs[:, 0, t, :],
                                              r1[:, bass.ds(c * TT + t, 1), :].rearrange("p a e -> p (a e)"),
                                              score[:, bass.ds(c * TT + t, 1)], None, ALU.mult
                                              ).then_inc(o_rows, 1)
                        dve.wait_ge(o_xT_full, i + 1)
                        dve.tensor_copy(xsT_o, bank[2][:, :].rearrange("p (k c) -> p k c", k=KE)
                                        ).then_inc(o_xT, 1)
                        for f in range(KF):
                            dve.wait_ge(o_gate, i * KF + f + 1)
                            dve.tensor_tensor(hT_o[:, f, :], bank[4][:, CAP:2 * CAP], gate[:, 0, :],
                                              ALU.mult).then_inc(o_h, 1)
                        dve.wait_ge(o_y, i + 1)
                        for t in range(TT):
                            rows = y_sh[:, bass.ds(c * TT + t, 1), :].rearrange("p a e -> p (a e)")
                            last = dve.scalar_tensor_tensor(
                                out=rows, in0=bank[0][:, t * E:(t + 1) * E],
                                scalar=over_mask[:, bass.ds(c * TT + t, 1), bass.ds(e, 1)].rearrange("p a b -> p (a b)"),
                                in1=rows, op0=ALU.mult, op1=ALU.add)
                        last.then_inc(o_sum, 1)
                        dve.wait_ge(o_sum, i + 2)
                over_links = [0]

                def over_link(ins):
                    over_links[0] += 1
                    ins.then_inc(o_link, 1)
                    dve.wait_ge(o_link, over_links[0])

                for c in range(CHUNKS):
                    last = moments(c, over_link)
                over_link(last)
            dve.tensor_scalar(mv[:, :, 1], mv[:, :, 1], EPS, None, ALU.add).then_inc(var2, 1)
            dve.wait_ge(std2, 1)
            link(dve.reciprocal(rstd[:, :], std[:, :]))
            for t in range(NT):
                dve.tensor_scalar(back[:, t, :], y_sh[:, t, :], mv[:, t, 0:1], rstd[:, t:t + 1],
                                  ALU.subtract, ALU.mult).then_inc(done, 1)

        @block.tensor
        def _(pe):
            def scores(p):
                b, u = divmod(p, PAIRS)
                kv = u // (PAIRS // HKV)
                s = SCORES[p % 2]
                if p >= 2:
                    pe.wait_ge(exp_ready, 4 * (p - 1))
                if u == 0:
                    pe.wait_ge(qT_act, 2 * b + 2)
                    pe.wait_ge(qT_dve, 2 * b + 2)
                    pe.wait_ge(kT_ready, 2 * b + 2)
                pe.matmul(bank[s][:, :], q4T[:, b % 2, u, P:L],
                          kbd[:, b % 2, kv, :, :].rearrange("p h k -> p (h k)"), start=True, stop=False)
                pe.matmul(bank[s][:, :].rearrange("p (h k) -> p h k", h=2)[:, :, P:L], ident_b, mask2,
                          start=False, stop=True)
                pe.matmul(bank[s + 1][:, 0:2 * P].rearrange("p (h k) -> p h k", h=2), q4T[:, b % 2, u, 0:P],
                          kbd[:, b % 2, kv, :, 0:P], start=True, stop=False)
                pe.matmul(bank[s + 1][:, 0:2 * P].rearrange("p (h k) -> p h k", h=2), ident_b, mask2,
                          start=False, stop=True).then_inc(scores_full, 1)

            def transpose_probs(p, j):
                pe.wait_ge(exp_ready, 4 * p + 2 * j + 2)
                if p:
                    pe.wait_ge(pt_ev[j], p)
                pr = probs[:, p % 2, j, :]
                for dst, src in ((0, L), (P, 0), (2 * P, P)):
                    last = pe.transpose(bank[PT[j]][:, dst:dst + P], pr[:, src:src + P], ident)
                last.then_inc(pt_full, 1)

            def weigh_values(g):
                b = g // GB
                kv = (g % GB) // (GB // HKV)
                pe.wait_ge(pt_ev[0], 2 * g + 2)
                pe.wait_ge(pt_ev[1], 2 * g + 2)
                if g:
                    pe.wait_ge(o_ev, g)
                if g % GB == 0:
                    pe.wait_ge(v_ready, TT * (b + 1))
                for k, src, dst in ((0, 0, 0), (1, L, P)):
                    for j in range(4):
                        last = pe.matmul(bank[OT][32 * j:32 * j + 32, dst:L], v_s[:, b % 2, k, kv, :],
                                         probsT[:, g % 2, j, src:src + L - dst], start=(k == 0), stop=(k == 1))
                last.then_inc(pv_done, 1)

            def misc(use):
                kind, b, i = use
                at = use_at[use]
                if at:
                    pe.wait_ge(misc_free, at)
                bk = bank[MISC]
                if kind == "proj":
                    for k in range(KE):
                        last = pe.matmul(bk[:, 0:NQKV], xT_s[:, k, (b * TT + i) * P:(b * TT + i + 1) * P],
                                         wqkv_s[:, k, :], start=(k == 0), stop=(k == KE - 1))
                elif kind == "qT":
                    t, half = divmod(i, 2)
                    pe.wait_ge(q_low, 2 * (b * TT + t) + 2)
                    for a in range(4):
                        h = 2 * (4 * half + a)
                        last = pe.transpose(bk[:, a * P:(a + 1) * P],
                                            q4[:, t, h:h + 2, :, :].bitcast(FP32).rearrange("p h s d -> p (h s d)"),
                                            ident)
                elif kind == "kT":
                    for t in range(TT):
                        for h in range(HKV):
                            at2 = t * HKV + h
                            last = pe.transpose(bk[:, at2 * P:(at2 + 1) * P],
                                                k4[:, t, h, :, :, :].bitcast(FP32).rearrange("p a s d -> p (a s d)"),
                                                ident)
                elif kind == "otr":
                    pe.wait_ge(o_ev, GB * (b + 1))
                    for g in range(GB):
                        last = pe.transpose(bk[:, g * P:(g + 1) * P], oT_s[:, g, i * P:(i + 1) * P], ident)
                elif kind == "onT":
                    pe.wait_ge(on_ready, TT * (b + 1))
                    for t in range(TT):
                        for k in range(KE):
                            at2 = t * KE + k
                            last = pe.transpose(bk[:, at2 * P:(at2 + 1) * P],
                                                on[:, t, 8 * k:8 * k + 8, :].rearrange("p h d -> p (h d)"), ident)
                else:
                    pe.wait_ge(onT_ready, b + 1)
                    for t in range(TT):
                        for k in range(KE):
                            last = pe.matmul(bk[:, t * E:(t + 1) * E], onT_s[:, t, k, :], wo_s[:, k, :],
                                             start=(k == 0), stop=(k == KE - 1))
                last.then_inc(misc_full, 1)

            pe.wait_ge(ld_x, 32)
            for use in first_uses:
                if use[0] == "qT":
                    pe.wait_ge(ld_c, 16 * 5)
                misc(use)
            pe.wait_ge(init, 2)
            pe.wait_ge(masks_ready, 1)
            scores(0)
            scores(1)
            pe.wait_ge(ld_w, 32)
            for p in range(NP):
                transpose_probs(p, 0)
                if p + 2 < NP:
                    scores(p + 2)
                transpose_probs(p, 1)
                if p % 2 == 0 and p:
                    weigh_values(p // 2 - 1)
                for use in slot_uses[p]:
                    misc(use)
            weigh_values(NG - 1)
            for use in slot_uses[NP]:
                misc(use)

            for c in range(NT // 2):
                pe.wait_ge(x1_ready, 2 * c + 2)
                if c >= 2:
                    pe.wait_ge(x1T_low, c - 1)
                for k in range(KE):
                    for t in range(2):
                        last = pe.transpose(bank[c % 2][:, (2 * k + t) * P:(2 * k + t + 1) * P],
                                            r1[:, 2 * c + t, k * P:(k + 1) * P], ident)
                last.then_inc(x1T_full, 1)
            pe.wait_ge(rw_ready, 1)
            pe.wait_ge(x1T_low, NT // 2)
            for t in range(NT):
                o = bank[2][:, t * 2 * NX:(t + 1) * 2 * NX]
                for k in range(KE):
                    pe.matmul(o, x1T_h[:, k, t * P:(t + 1) * P], rw_r[:, k, :, :].rearrange("p s e -> p (s e)"),
                              start=(k == 0), stop=False)
                for k in range(KE):
                    last = pe.matmul(o[:, 0:NX], x1T_l[:, k, t * P:(t + 1) * P], rw_r[:, k, 0, :],
                                     start=False, stop=(k == KE - 1))
            last.then_inc(logits_full, 1)

            def products(n):
                if chunk_of(n) is not None:
                    c = slice(chunk_of(n) * CAP, (chunk_of(n) + 1) * CAP)
                    return [(x1T_h[:, k, c], x1T_l[:, k, c]) for k in range(KE)]
                e = n - SH1
                return [(xsT_h[:, e % 2, k, :], xsT_l[:, e % 2, k, :]) for k in range(KE)]

            def weights(s, q):
                if s < EARLY:
                    pe.wait_ge(early_low, 4 * s + q + 1)
                else:
                    pe.wait_ge(w_low_dve, split_count(s, q))
                    pe.wait_ge(w_low_pool, split_count(s, q))

            def gate_up(n, f):
                i = n * KF + f
                par = set_of(n) % RING
                if f == 0:
                    weights(set_of(n), 2)
                    if chunk_of(n) is None:
                        pe.wait_ge(xsT_low, n - SH1 + 1)
                if i >= 4:
                    pe.wait_ge(h_ready, i - 3)
                xt = products(n)
                for up in range(2):
                    o = bank[4 + i % 4][:, up * CAP:(up + 1) * CAP]
                    for k in range(KE):
                        pe.matmul(o, gu(par, True, f, k, up), xt[k][0], start=(k == 0), stop=False)
                        pe.matmul(o, gu(par, True, f, k, up), xt[k][1], start=False, stop=False)
                        last = pe.matmul(o, gu(par, False, f, k, up), xt[k][0], start=False, stop=(k == KE - 1))
                last.then_inc(gu_full, 1)

            def down_rows(n):
                par = set_of(n) % RING
                pe.wait_ge(h_low, (n + 1) * KF)
                weights(set_of(n), 3)
                if n >= 2:
                    if chunk_of(n - 2) is None:
                        pe.wait_ge(ys_ready, n - 1 - SH1)
                    else:
                        pe.wait_ge(y_sh_ready, chunk_of(n - 2) + 1)
                for t in range(TT):
                    o = bank[n % 2][:, t * E:(t + 1) * E]
                    c = slice(t * P, (t + 1) * P)
                    for f in range(KF):
                        pe.matmul(o, hT_h[:, n % 2, f, c], down(par, True, f), start=(f == 0), stop=False)
                        pe.matmul(o, hT_h[:, n % 2, f, c], down(par, False, f), start=False, stop=False)
                        last = pe.matmul(o, hT_l[:, n % 2, f, c], down(par, True, f), start=False,
                                         stop=(f == KF - 1))
                last.then_inc(y_full, 1)

            def rows_T(e):
                pe.wait_ge(xs_in[e % 2], 16 * (e // 2 + 1))
                if e >= 2:
                    pe.wait_ge(xsT_low, e - 1)
                for k in range(KE):
                    for t in range(TT):
                        last = pe.transpose(bank[2 + e % 2][:, k * CAP + t * P:k * CAP + (t + 1) * P],
                                            xs[:, e % 2, t, k * P:(k + 1) * P], ident)
                last.then_inc(xsT_full, 1)

            for n in range(NB):
                for f in range(KF):
                    gate_up(n, f)
                    if n == 0 and f == 0:
                        pe.wait_ge(onehot_ready, 1)
                        o = bank[3][:, 0:NT * NX].rearrange("p (t e) -> p t e", t=NT)
                        pe.matmul(o, earlier, onehot_b[:, :, :], start=True, stop=False)
                        for s in range(1, NT):
                            last = pe.matmul(o[:, s:NT, :], ones_b, onehot_b[:, 0:NT - s, :], start=False,
                                             stop=(s == NT - 1))
                        last.then_inc(rank_full, 1)
                    if n == 0 and f == 1:
                        pe.wait_ge(over_ready, 1)
                        pe.matmul(bank[3][:, NT * NX:NT * NX + NT], ones_b, over_b[:, :], start=True,
                                  stop=True).then_inc(over_full, 1)
                    if f == 0 and n:
                        down_rows(n - 1)
                    if f == 1 and SH1 <= n + 1 < SH2:
                        rows_T(n + 1 - SH1)
            down_rows(NB - 1)
            with overflow(pe):
                with pe.Fori(0, NX) as e, pe.Fori(0, CHUNKS) as c:
                    i = e * CHUNKS + c
                    pe.wait_ge(o_rows, i * TT + TT)
                    for k in range(KE):
                        for t in range(TT):
                            last = pe.transpose(bank[2][:, k * CAP + t * P:k * CAP + (t + 1) * P],
                                                xs[:, 0, t, k * P:(k + 1) * P], ident)
                    last.then_inc(o_xT_full, 1)
                    pe.wait_ge(o_xT, i + 1)
                    pe.wait_ge(o_w, e * 32 + 32)
                    g, d = w_raw[:, 0, part_of(0)], w_raw[:, 0, part_of(1)]
                    g, d = g.rearrange("p (k n) -> p k n", k=KE), d.rearrange("p (f n) -> p f n", f=KF)
                    for f in range(KF):
                        pe.wait_ge(o_h, i * KF + f + 1)
                        for up in range(2):
                            for k in range(KE):
                                n = up * F + f * P
                                last = pe.matmul(bank[4][:, up * CAP:(up + 1) * CAP], g[:, k, n:n + P],
                                                 xsT_o[:, k, :], start=(k == 0), stop=(k == KE - 1))
                        last.then_inc(o_gu, 1)
                    pe.wait_ge(o_h, i * KF + KF + 1)
                    for t in range(TT):
                        for f in range(KF):
                            last = pe.matmul(bank[0][:, t * E:(t + 1) * E], hT_o[:, f, t * P:(t + 1) * P],
                                             d[:, f, :], start=(f == 0), stop=(f == KF - 1))
                    last.then_inc(o_y, 1)


def constants():
    half = np.arange(HALF, dtype=np.float32) / np.float32(HALF)
    inv = (np.float32(THETA) ** (-half)).astype(np.float32)
    ang = np.arange(L, dtype=np.float32)[:, None] * inv[None, :]
    cos, sin = np.cos(ang).astype(np.float32), np.sin(ang).astype(np.float32)
    scale = np.where(np.arange(HR) < HQ, np.float32(D ** -0.5), np.float32(1.0)).astype(np.float32)
    cosq = np.concatenate([cos, cos], 1)[:, None, :] * scale[None, :, None]
    sinq = np.concatenate([-sin, sin], 1)[:, None, :] * scale[None, :, None]
    eye = np.eye(P, dtype=np.float32)
    cf = np.concatenate([eye, np.tile(np.arange(NX, dtype=np.float32), (P, 1))], 1)
    k, q = np.arange(P)[None, :], np.arange(P)[:, None]
    mask = np.where(k > q, np.float32(MASKED), np.float32(0))
    earlier = (q < k).astype(np.float32)
    cb = np.concatenate([eye, mask, mask, earlier, np.ones((P, P), np.float32)], 1)
    return cosq.reshape(L, HR * D), sinq.reshape(L, HR * D), cf, cb


def kernel(**inputs):
    import concourse.bacc as bacc
    from concourse.bass_utils import run_bass_kernel_spmd

    a = {n: np.asarray(v) for n, v in inputs.items()}
    x = a["L0_attn_x"].reshape(T, E)
    cosq, sinq, cf, cb = constants()
    arrays = {
        "x": x,
        "xT": x.T,
        "wqkvT": np.concatenate([a["L0_attn_wq"], a["L0_attn_wk"], a["L0_attn_wv"]], 0).T,
        "bqkv": np.concatenate([a["L0_attn_bq"], a["L0_attn_bk"], a["L0_attn_bv"]])[None, :],
        "woT": a["L0_attn_wo"].T,
        "rwT": a["L0_ffn_router_w"].T,
        "wgu": a["L0_ffn_gate_up_proj"],
        "wd": a["L0_ffn_down_proj"],
        "swg": a["L0_ffn_shared_gate_w"],
        "swu": a["L0_ffn_shared_up_w"],
        "swd": a["L0_ffn_shared_down_w"],
        "cosq": cosq, "sinq": sinq, "cf": cf, "cb": cb,
    }
    arrays = {n: np.ascontiguousarray(v) for n, v in arrays.items()}
    nc = bacc.Bacc("TRN2", target_bir_lowering=False, num_devices=1)
    args = [nc.dram_tensor(n, v.shape, mybir.dt.from_np(v.dtype), kind="ExternalInput").ap()
            for n, v in arrays.items()]
    out = nc.dram_tensor("out", (T, E), FP32, kind="ExternalOutput").ap()
    program(nc, *args, out)
    r = run_bass_kernel_spmd(nc, [arrays], core_ids=[0])
    return r.results[0]["out"].reshape(B, L, E)
```

```python
import numpy as np
import concourse.bass as bass
from concourse import mybir
from contextlib import ExitStack

FP32 = mybir.dt.float32
FP32R = mybir.dt.float32r
BF16 = mybir.dt.bfloat16
U32 = mybir.dt.uint32
I32 = mybir.dt.int32
ALU = mybir.AluOpType
ACT = mybir.ActivationFunctionType
AX = mybir.AxisListType

P = 128
B, L, E = 4, 256, 256
T = B * L
NT = T // P
KE = E // P
HQ, HKV, D = 16, 2, 16
HALF = D // 2
HR = HQ + HKV
NQKV = (HQ + 2 * HKV) * D
NX, F = 8, 512
KF = F // P
TT = L // P
PAIRS = HQ // 2
NP = B * PAIRS
GB = HQ // 4
CAP = 256
NSLOT = NX * CAP
THETA = 10000.0
EPS = 1e-5
WARM = {"loads": 5, "rotation": 12, "first queries": 4, "layer norm": 13}
MASKED = -1.0e30
WSET = KE * 2 * F + KF * E
NSETS = NX + 2
CHUNKS = T // CAP
SH1 = CHUNKS // 2
NB = CHUNKS + NX
SH2 = SH1 + NX
RAW = 3
RING = 3
EARLY = 2
EARLY_AFTER = (0, 0, 2, 5, 8)
QUARTER = WSET // 4


def aux_uses():
    slots = [[] for _ in range(NP + 2)]
    for b in range(B):
        at = PAIRS * b
        for g in range(GB):
            slots[at + 2 * g + 2] += [("pv", b, g)]
        if b == 0:
            for i, use in ((0, ("proj", 1, 0)), (0, ("proj", 1, 1)), (2, ("qT", 1, 0)), (3, ("qT", 1, 1)),
                           (4, ("qT", 1, 2)), (5, ("qT", 1, 3)), (5, ("kT", 1, 0))):
                slots[i] += [use]
        elif b + 1 < B:
            for i, use in ((-3, ("proj", b + 1, 0)), (0, ("proj", b + 1, 1)), (1, ("qT", b + 1, 0)),
                           (1, ("qT", b + 1, 1)), (2, ("qT", b + 1, 2)), (3, ("qT", b + 1, 3)), (3, ("kT", b + 1, 0))):
                slots[at + i] += [use]
        if 0 < b < B - 1:
            for i, use in ((4, ("otr", b - 1, 0)), (5, ("otr", b - 1, 1)), (7, ("onT", b - 1, 0)),
                           (9, ("wo", b - 1, 0))):
                slots[at + i] += [use]
        elif b:
            for i, use in ((2, ("otr", b - 1, 0)), (4, ("otr", b - 1, 1)), (5, ("onT", b - 1, 0)),
                           (6, ("wo", b - 1, 0))):
                slots[at + i] += [use]
    slots.pop()
    first = [("proj", 0, 0), ("proj", 0, 1), ("kT", 0, 0), ("qT", 0, 0), ("qT", 0, 2)]
    second = [("qT", 0, 1), ("qT", 0, 3)]
    last = [(kind, B - 1, t) for kind in ("otr", "onT", "wo") for t in range(TT)]
    order = first + second + [u for s in slots for u in s] + last
    return first, second, slots, last, order, {u: i for i, u in enumerate(order)}


def tiles_of(use):
    _, b, i = use
    return range(TT) if b < B - 1 else range(i, i + 1)


def outputs_done(use):
    _, b, i = use
    return b + 1 + i


def set_of(block):
    return min(max(block - SH1 + 1, 0), NSETS - 1)


def chunk_of(block):
    return block if block < SH1 else block - NX if block >= SH2 else None


def last_block(s):
    return SH1 - 1 + s


def part_of(part):
    return slice(0, KE * 2 * F) if part == 0 else slice(KE * 2 * F, WSET)


def quarter(q, half=None):
    if half is None:
        return slice(q * QUARTER, (q + 1) * QUARTER)
    return slice(q * QUARTER + half * QUARTER // 2, q * QUARTER + (half + 1) * QUARTER // 2)


def split_with(block):
    if block == SH1 - 1:
        return EARLY
    s = set_of(block) + 1
    return s if EARLY < s < NSETS and set_of(block + 1) == s else None


def rows_late(block):
    return block in (SH1 - 1, NB - 1)


def raw_loaded(s):
    return 16 * sum(3 if r in (0, NSETS - 1) else 2 for r in range(s % RAW, s + 1, RAW))


def split_count(s, q):
    return 4 * (s - EARLY) + q + 1


def program(nc, x, xT, wqkvT, bqkv, woT, rwT, wgu, wd, swg, swu, swd, cos, sin, cf, mask, out):
    first_uses, second_uses, slot_uses, last_uses, uses, use_at = aux_uses()
    xs_dram = nc.dram_tensor("xs_dram", (NSLOT, E), FP32).ap()
    ys_dram = nc.dram_tensor("ys_dram", (NSLOT, E), FP32).ap()

    ctx = ExitStack()
    with ctx:
        def sb(name, shape, dt=FP32):
            return ctx.enter_context(nc.sbuf_tensor(name, shape, dt))

        def sem(name):
            return ctx.enter_context(nc.semaphore(name))

        cf_s = sb("cf_s", [P, P + 2 * NX])
        cb_s = sb("cb_s", [P, 5 * P], BF16)
        ident = cf_s[:, 0:P]
        expert_no = cf_s[:, P:P + NX]
        sum_parts = cf_s[0:2 * NX, P + NX:]
        ident_b = cb_s[:, 0:P]
        mask2 = cb_s[:, P:3 * P].rearrange("p (a k) -> p a k", a=2)
        earlier = cb_s[:, 3 * P:4 * P]
        ones_b = cb_s[:, 4 * P:5 * P]
        r1 = sb("r1", [P, NT, E])
        idle = sb("idle", [P, 4 * P], BF16)
        rw_s = sb("rw_s", [P, KE, NX])
        rw_r = sb("rw_r", [P, KE, 2, NX], FP32R)

        stats = sb("stats", [P, NT, 6])
        mv = sb("mv", [P, NT, 2])
        std = sb("std", [P, NT])
        rstd = sb("rstd", [P, NT])
        shift = sb("shift", [P, NT])
        lg = sb("lg", [P, NT, NX])
        top = sb("top", [P, NT])
        pick = sb("pick", [P, NT, NX])
        first = sb("first", [P, NT])
        onehot = sb("onehot", [P, NT, NX])
        onehot_b = sb("onehot_b", [P, NT, NX], BF16)
        score = sb("score", [P, NT])
        place = sb("place", [P, NT, NX])
        rank = sb("rank", [P, NT])
        slot_f = sb("slot_f", [P, NT])
        over = sb("over", [P, NT])
        over_b = sb("over_b", [P, NT], BF16)
        over_mask = sb("over_mask", [P, NT, NX])
        n_over_f = sb("n_over_f", [P, 1])
        n_over = sb("n_over", [P, 1], I32)
        slot_u = sb("slot_u", [P, NT], U32)
        zero = sb("zero", [P, E])

        w_raw = sb("w_raw", [P, RAW, WSET])
        w_h = [sb(f"w_h{i}", [P, WSET], FP32R) for i in range(EARLY)]
        w_l = [sb(f"w_l{i}", [P, WSET], FP32R) for i in range(EARLY)]

        attention = ExitStack()

        def early(name, shape, dt=FP32):
            return attention.enter_context(nc.sbuf_tensor(name, shape, dt))

        xT_s = early("xT_s", [P, KE, T])
        wqkv_s = early("wqkv_s", [P, KE, NQKV])
        bias_s = early("bias_s", [P, NQKV])
        wo_s = early("wo_s", [P, KE, E])
        cos_s = early("cos_s", [P, TT, D])
        sin_s = early("sin_s", [P, TT, 2, HALF])
        qkv = early("qkv", [P, TT, NQKV])
        rot_c = early("rot_c", [P, TT, HR, D])
        rot_s = early("rot_s", [P, TT, HR, 2, HALF])
        rot = early("rot", [P, TT, HR, D])
        q4 = early("q4", [P, TT, HQ, 4, D], FP32R)
        k4 = early("k4", [P, TT, HKV, 4, 2, D], FP32R)
        q4T = early("q4T", [P, 2, PAIRS, L], FP32R)
        kbd = early("kbd", [P, 2, HKV, 2, L], FP32R)
        v_s = early("v_s", [P, 3, TT, HKV, 2 * D])
        negmax = early("negmax", [P, B, TT, HQ])
        rdenom = early("rdenom", [P, TT, HQ])
        probs = early("probs", [P, 2, 2, L + P])
        probsT = early("probsT", [P, 2, 4, L + P])
        oT_s = early("oT_s", [P, 2, GB, L])
        on = early("on", [P, TT, HQ, D])
        onT_s = early("onT_s", [P, TT, KE, P])

        attention.close()

        x1T_h = sb("x1T_h", [P, KE, T], FP32R)
        x1T_l = sb("x1T_l", [P, KE, T], FP32R)
        x1s = sb("x1s", [P, NT, E])
        w_h += [sb(f"w_h{i}", [P, WSET], FP32R) for i in range(EARLY, RING)]
        w_l += [sb(f"w_l{i}", [P, WSET], FP32R) for i in range(EARLY, RING)]
        lgT = sb("lgT", [2 * NX, T])
        xs = sb("xs", [P, 2, TT, E])
        ys = sb("ys", [P, 2, TT, E])
        xsT_h = sb("xsT_h", [P, 2, KE, CAP], FP32R)
        xsT_l = sb("xsT_l", [P, 2, KE, CAP], FP32R)
        gate = sb("gate", [P, 2, CAP])
        hT = sb("hT", [P, 2, CAP])
        hT_h = sb("hT_h", [P, 2, KF, CAP], FP32R)
        hT_l = sb("hT_l", [P, 2, KF, CAP], FP32R)
        y_sh = sb("y_sh", [P, NT, E])
        back = sb("back", [P, NT, E])

        bank = [ctx.enter_context(nc.psum_tensor(f"bank{i}", [P, 512], FP32)) for i in range(8)]
        SCORES, PT, AUX, X1 = [0, 2], [4, 5], [6, 7], [0, 1, 4, 5]

        mask_f = probs[:, :, :, :].rearrange("p a j q -> p (a j q)")[:, 0:P]
        spare = w_raw[:, 1, :]
        xsT_o = spare[:, 0:KE * CAP].rearrange("p (k c) -> p k c", k=KE)
        hT_o = spare[:, KE * CAP:(KE + KF) * CAP].rearrange("p (f c) -> p f c", f=KF)

        ld_c, ld_x, ld_w, ld_r = sem("ld_consts"), sem("ld_x"), sem("ld_wo"), sem("ld_tok")
        raw_in = [sem(f"raw_in{i}") for i in range(RAW)]
        init, masks_ready = sem("init"), sem("masks_ready")
        aux_full = sem("aux_full")
        rope_in, rope_cos, rope_sin, rope_sum, q_high, q_low = (
            sem("rope_in"), sem("rope_cos"), sem("rope_sin"), sem("rope_sum"), sem("q_high"), sem("q_low"))
        v_ready = sem("v_ready")
        qT_act, qT_dve = sem("qT_act"), sem("qT_dve")
        kT_ready = sem("kT_ready")
        scores_full, max_ready, exp_ready = sem("scores_full"), sem("max_ready"), sem("exp_ready")
        pt_full, pt_ev = sem("pt_full"), [sem("pt_ev0"), sem("pt_ev1")]
        o_ev = sem("o_ev")
        on_ready, onT_ready, r1_ready = sem("on_ready"), sem("onT_ready"), sem("r1_ready")
        dve_link = sem("dve_link")
        var_ready, std_ready, x1_ready = sem("var_ready"), sem("std_ready"), sem("x1_ready")
        x1T_full, x1T_high, x1T_low = sem("x1T_full"), sem("x1T_high"), sem("x1T_low")
        rw_ready = sem("rw_ready")
        logitsT_full, lgT_act, lgT_dve = sem("logitsT_full"), sem("lgT_act"), sem("lgT_dve")
        shift_ready, x1_act, shift2_ready = sem("shift_ready"), sem("x1_act"), sem("shift2_ready")
        done_act, warm_ready, joined = sem("done_act"), sem("warm_ready"), sem("joined")
        logits_full, onehot_ready, rank_full = sem("logits_full"), sem("onehot_ready"), sem("rank_full")
        top_ready, score_ready, slot_ready = sem("top_ready"), sem("score_ready"), sem("slot_ready")
        scaled, zeroed = sem("scaled"), sem("zeroed")
        zero_rows = sem("zero_rows")
        scattered = sem("scattered")
        w_high, w_low_dve, w_low_pool = sem("w_high"), sem("w_low_dve"), sem("w_low_pool")
        early_high, early_low = sem("early_high"), sem("early_low")
        xs_in = [sem("xs_in0"), sem("xs_in1")]
        xsT_full, xsT_high, xsT_low = sem("xsT_full"), sem("xsT_high"), sem("xsT_low")
        gu_full, gate_ready, h_ready, h_high, h_low = (
            sem("gu_full"), sem("gate_ready"), sem("h_ready"), sem("h_high"), sem("h_low"))
        y_full, y_sh_ready, ys_ready = sem("y_full"), sem("y_sh_ready"), sem("ys_ready")
        ys_out = [sem("ys_out0"), sem("ys_out1")]
        got = [sem(f"got{t}") for t in range(NT)]
        var2, std2, done = sem("var2"), sem("std2"), sem("done")
        stored = sem("stored")
        over_ready, over_full, n_over_ready = sem("over_ready"), sem("over_full"), sem("n_over_ready")
        back_zero = sem("back_zero")
        o_w, o_rows, o_xT_full, o_xT, o_gu, o_gate, o_h, o_y, o_sum, o_link = (
            sem("o_weights"), sem("o_rows"), sem("o_xT_full"), sem("o_xT"), sem("o_gate_up"),
            sem("o_gate"), sem("o_h"), sem("o_y"), sem("o_sum"), sem("o_link"))
        block = ctx.enter_context(nc.Block())

        def gu(par, high, f, k, up):
            w = (w_h if high else w_l)[par][:, 0:KE * 2 * F].rearrange("p (k n) -> p k n", k=KE)
            return w[:, k, up * F + f * P:up * F + (f + 1) * P]

        def down(par, high, f):
            w = (w_h if high else w_l)[par][:, KE * 2 * F:].rearrange("p (f n) -> p f n", f=KF)
            return w[:, f, :]

        def aux(use):
            return bank[AUX[use_at[use] % 2]]

        def weighed(g):
            return use_at[("pv", g // GB, g % GB)] + 1

        def read_over(eng):
            eng.wait_ge(n_over_ready, 1)
            return eng.value_load(n_over[0:1, 0:1], min_val=0, max_val=T)

        @block.sync
        def _(sp):
            sp.dma_start(wqkv_s[:, :, :], wqkvT.rearrange("(k p) n -> p k n", p=P)).then_inc(ld_x, 16)
            xTv = xT.rearrange("(k p) t -> p k t", p=P)
            sp.dma_start(xT_s[:, :, 0:L], xTv[:, :, 0:L]).then_inc(ld_x, 16)
            sp.wait_ge(ld_x, 32)
            sp.wait_ge(ld_c, 16 * 5)
            sp.dma_start(xT_s[:, :, L:T], xTv[:, :, L:T]).then_inc(ld_w, 16)
            sp.dma_start(wo_s[:, :, :], woT.rearrange("(k p) n -> p k n", p=P)).then_inc(ld_w, 16)
            sp.dma_start(r1[:, :, :], x.rearrange("(t p) e -> p t e", p=P)).then_inc(ld_r, 16)
            sp.dma_start(rw_s[:, :, :], rwT.rearrange("(k p) n -> p k n", p=P)).then_inc(ld_r, 16)
            def load_set(s):
                if s >= RAW:
                    if s - RAW < EARLY:
                        sp.wait_ge(early_low, 4 * (s - RAW) + 4)
                    else:
                        sp.wait_ge(w_low_dve, split_count(s - RAW, 3))
                        sp.wait_ge(w_low_pool, split_count(s - RAW, 3))
                r = w_raw[:, s % RAW, :]
                g, d = r[:, 0:KE * 2 * F].rearrange("p (k n) -> p k n", k=KE), r[:, KE * 2 * F:]
                if s in (0, NSETS - 1):
                    sp.dma_start(g[:, :, 0:F], swg.rearrange("(k p) n -> p k n", p=P)).then_inc(raw_in[s % RAW], 16)
                    sp.dma_start(g[:, :, F:], swu.rearrange("(k p) n -> p k n", p=P)).then_inc(raw_in[s % RAW], 16)
                    src = swd
                else:
                    sp.dma_start(g, wgu[s - 1].rearrange("(k p) n -> p k n", p=P)).then_inc(raw_in[s % RAW], 16)
                    src = wd[s - 1]
                sp.dma_start(d.rearrange("p (f n) -> p f n", f=KF),
                             src.rearrange("(f p) n -> p f n", p=P)).then_inc(raw_in[s % RAW], 16)

            for s in range(RAW):
                load_set(s)
            sp.wait_ge(zeroed, 1)
            sp.dma_start(xs_dram.rearrange("(n p) d -> p n d", p=P),
                         zero[:, :].unsqueeze(1).broadcast_to((P, NSLOT // P, E))).then_inc(zero_rows, 16)
            load_set(RAW)

            def store_rows(e):
                sp.wait_ge(ys_ready, e + 1)
                sp.dma_start(ys_dram[e * CAP:(e + 1) * CAP, :].rearrange("(t p) d -> p t d", p=P),
                             ys[:, e % 2, :, :]).then_inc(ys_out[e % 2], 16)

            def load_rows(e):
                if e >= 2:
                    sp.wait_ge(xsT_full, e - 1)
                sp.dma_start(xs[:, e % 2, :, :],
                             xs_dram[e * CAP:(e + 1) * CAP, :].rearrange("(t p) d -> p t d", p=P)
                             ).then_inc(xs_in[e % 2], 16)

            sp.wait_ge(scattered, 16 * NT)
            load_rows(0)
            load_rows(1)
            n_over_sp = read_over(sp)
            for e in range(NX):
                if e + 2 < NX:
                    load_rows(e + 2)
                if e >= 2:
                    store_rows(e - 2)
                if e + 4 < NSETS:
                    load_set(e + 4)
            store_rows(NX - 2)
            store_rows(NX - 1)
            with sp.If(n_over_sp > 0):
                with sp.Fori(0, NX) as e:
                    sp.wait_ge(o_sum, e * CHUNKS + 1)
                    g, d = w_raw[:, 0, part_of(0)], w_raw[:, 0, part_of(1)]
                    sp.dma_start(g.rearrange("p (k n) -> p k n", k=KE),
                                 wgu[bass.ds(e, 1)].rearrange("a (k p) n -> p (a k) n", p=P)).then_inc(o_w, 16)
                    sp.dma_start(d.rearrange("p (f n) -> p f n", f=KF),
                                 wd[bass.ds(e, 1)].rearrange("a (f p) n -> p (a f) n", p=P)).then_inc(o_w, 16)
            for i, t in enumerate((*range(TT), *range(NT - TT, NT))):
                if i == TT:
                    for u in range(TT, NT - TT):
                        sp.wait_ge(done_act, u - TT + 1)
                        sp.dma_start(out[u * P:(u + 1) * P, :], back[:, u, :]).then_inc(stored, 16)
                sp.wait_ge(done, i + 1)
                sp.dma_start(out[t * P:(t + 1) * P, :], back[:, t, :]).then_inc(stored, 16)
            sp.wait_ge(stored, 16 * NT)

        @block.gpsimd
        def _(pool):
            pool.memset(zero[:, :], 0.0).then_inc(zeroed, 1)
            pool.memset(kbd[:, :, :, :, :].bitcast(FP32), 0.0).then_inc(init, 1)
            pool.memset(v_s[:, :, :, :, :], 0.0).then_inc(init, 1)
            pool.wait_ge(init, 2)
            pool.memset(v_s[:, :, :, :, D:D + 1], 1.0).then_inc(init, 1)
            pool.memset(ones_b, 1.0).then_inc(init, 1)
            pool.wait_ge(init, 4)
            pool.wait_ge(ld_c, 16 * 5)

            def split_early(s, q):
                c = quarter(q)
                pool.wait_ge(raw_in[s], raw_loaded(s))
                pool.tensor_tensor(w_h[s][:, c].rearrange("p (n e) -> p n e", e=E),
                                   w_raw[:, s, c].rearrange("p (n e) -> p n e", e=E),
                                   zero[:, :].unsqueeze(1).broadcast_to((P, QUARTER // E, E)),
                                   ALU.add).then_inc(early_high, 1)
                pool.wait_ge(early_high, 4 * s + q + 1)
                pool.tensor_tensor(w_l[s][:, c], w_raw[:, s, c], w_h[s][:, c].bitcast(FP32),
                                   ALU.subtract).then_inc(early_low, 1)

            early_quarters = [(s, q) for s in range(EARLY) for q in range(4)]
            def rope(b, t):
                i = b * TT + t
                pool.wait_ge(rope_in, i + 1)
                if i >= TT:
                    pool.wait_ge(rope_sum, i - TT + 1)
                qk = qkv[:, t, 0:HR * D].rearrange("p (h s d) -> p h s d", h=HR, s=2)
                sin_b = sin_s[:, t, :, :].unsqueeze(1).broadcast_to((P, HR, 2, HALF))
                pool.tensor_tensor(rot_s[:, t, :, 0, :], qk[:, :, 1, :], sin_b[:, :, 0, :],
                                   ALU.mult).then_inc(rope_sin, 1)
                pool.tensor_tensor(rot_s[:, t, :, 1, :], qk[:, :, 0, :], sin_b[:, :, 1, :],
                                   ALU.mult).then_inc(rope_sin, 1)
                if b:
                    pool.wait_ge(rope_cos, i + 1)
                    pool.wait_ge(rope_sin, 2 * i + 2)
                    pool.wait_ge(q_low, 2 * TT if b == 1 else 2 * (i - TT) + 2)
                    pool.wait_ge(q_high, 2 * (i - TT) + 2)
                    pool.tensor_tensor(rot[:, t, :, :], rot_c[:, t, :, :],
                                       rot_s[:, t, :, :, :].rearrange("p h s d -> p h (s d)"),
                                       ALU.add).then_inc(rope_sum, 1)
                if b >= 3:
                    pool.wait_ge(aux_full, weighed(GB * (b - 2) - 1))
                pool.tensor_copy(v_s[:, b % 3, t, :, 0:D],
                                 qkv[:, t, HR * D:].rearrange("p (h d) -> p h d", h=HKV)
                                 ).then_inc(v_ready, 1)
                pool.wait_ge(q_high, 2 * i + 2)
                if b:
                    pool.tensor_tensor(q4[:, t, :, 2:4, :],
                                       rot[:, t, 0:HQ, :].unsqueeze(2).broadcast_to((P, HQ, 2, D)),
                                       q4[:, t, :, 0:2, :].bitcast(FP32), ALU.subtract).then_inc(q_low, 1)
                pool.tensor_tensor(k4[:, t, :, :, 1, :],
                                   rot[:, t, HQ:, :].unsqueeze(2).broadcast_to((P, HKV, 4, D)),
                                   k4[:, t, :, :, 0, :].bitcast(FP32), ALU.subtract).then_inc(q_low, 1)

            for b in range(B):
                for t in range(TT):
                    rope(b, t)
                for s, q in early_quarters[EARLY_AFTER[b]:EARLY_AFTER[b + 1]]:
                    split_early(s, q)

            def split_low(s, q):
                pool.wait_ge(w_high, split_count(s, q))
                c = quarter(q, 1)
                pool.tensor_tensor(w_l[s % RING][:, c], w_raw[:, s % RAW, c],
                                   w_h[s % RING][:, c].bitcast(FP32), ALU.subtract).then_inc(w_low_pool, 1)

            pool.wait_ge(slot_ready, 1)
            pool.wait_ge(zero_rows, 16)
            for t in range(NT):
                pool.wait_ge(scaled, t + 1)
                pool.indirect_dma_start(xs_dram, bass.IndirectOffsetOnAxis(ap=slot_u[:, t:t + 1], axis=0),
                                        x1s[:, t, :], None, bounds_check=NSLOT - 1,
                                        oob_is_err=False).then_inc(scattered, 16)
            for s in range(EARLY, NSETS):
                for q in range(4):
                    split_low(s, q)
                if s == EARLY:
                    pool.memset(back[:, :, :], 0.0).then_inc(back_zero, 1)
            pool.wait_ge(back_zero, 1)
            pool.wait_ge(ys_out[0], 16 * (NX // 2))
            pool.wait_ge(ys_out[1], 16 * (NX // 2))
            for t in range(NT):
                pool.indirect_dma_start(back[:, t, :], None, ys_dram,
                                        bass.IndirectOffsetOnAxis(ap=slot_u[:, t:t + 1], axis=0),
                                        bounds_check=NSLOT - 1, oob_is_err=False).then_inc(got[t], 16)
            for t in range(SH1 * TT, NT):
                pool.wait_ge(got[t], 16)
                pool.tensor_tensor(y_sh[:, t, :], r1[:, t, :], back[:, t, :], ALU.add).then_inc(joined, 1)

        @block.scalar
        def _(act):
            act.dma_start(bias_s[:, :], bqkv.broadcast_to((P, NQKV))).then_inc(ld_c, 16)
            act.dma_start(cos_s[:, :, :], cos.rearrange("(t p) d -> p t d", p=P)).then_inc(ld_c, 16)
            act.dma_start(sin_s[:, :, :, :], sin.rearrange("(t p) (s d) -> p t s d", p=P, s=2)).then_inc(ld_c, 16)
            act.dma_start(cf_s[:, :], cf).then_inc(ld_c, 16)
            act.dma_start(mask_f, mask).then_inc(ld_c, 16)

            def high_parts(b, t):
                i = b * TT + t
                act.wait_ge(rope_sum, i + 1)
                if b:
                    act.wait_ge(aux_full, use_at[("kT", b - 1, 0)] + 1)
                act.activation(q4[:, t, :, 0:2, :], rot[:, t, 0:HQ, :].unsqueeze(2).broadcast_to((P, HQ, 2, D)),
                               ACT.Copy).then_inc(q_high, 1)
                act.activation(k4[:, t, :, :, 0, :], rot[:, t, HQ:, :].unsqueeze(2).broadcast_to((P, HKV, 4, D)),
                               ACT.Copy).then_inc(q_high, 1)

            def exps(p):
                b, u = divmod(p, PAIRS)
                act.wait_ge(max_ready, 2 * p + 2)
                if p >= 2:
                    act.wait_ge(pt_full, 2 * (p - 1))
                s = SCORES[p % 2]
                for j in range(2):
                    h = 2 * u + j
                    for t, src, dst in ((1, bank[s][:, j * L:(j + 1) * L], probs[:, p % 2, j, 0:L]),
                                        (0, bank[s + 1][:, j * P:(j + 1) * P], probs[:, p % 2, j, L:L + P])):
                        act.activation(dst, src, ACT.Exp, bias=negmax[:, b, t, h:h + 1]).then_inc(exp_ready, 1)

            def serve(use):
                kind, b, i = use
                bk = aux(use)
                if kind == "qT" and i % 2 == 0:
                    act.wait_ge(aux_full, use_at[use] + 1)
                    act.activation(q4T[:, b % 2, 0:4, (i // 2) * P:(i // 2 + 1) * P],
                                   bk[:, :].rearrange("p (a q) -> p a q", a=4), ACT.Copy).then_inc(qT_act, 1)
                elif kind == "kT":
                    act.wait_ge(aux_full, use_at[use] + 1)
                    for j in range(2):
                        act.activation(kbd[64 * j:64 * j + 64, b % 2, :, j, :].rearrange("p h (t k) -> p t h k", t=TT),
                                       bk[64 * j:64 * j + 64, :].rearrange("p (t h k) -> p t h k", t=TT, h=HKV),
                                       ACT.Copy, scale=D ** -0.5).then_inc(kT_ready, 1)
                elif kind == "onT":
                    act.wait_ge(aux_full, use_at[use] + 1)
                    a, z = tiles_of(use)[0], tiles_of(use)[-1] + 1
                    act.activation(onT_s[:, a:z, :, :].rearrange("p t k q -> p (t k q)"), bk[:, 0:(z - a) * E],
                                   ACT.Copy).then_inc(onT_ready, 1)
                elif kind == "pv":
                    act.wait_ge(aux_full, use_at[use] + 1)
                    act.activation(oT_s[:, b % 2, i, :], bk[:, 0:L], ACT.Copy).then_inc(o_ev, 1)

            for t in range(TT):
                high_parts(0, t)
            for use in first_uses:
                serve(use)
            exps(0)
            for p in range(NP):
                b, u = divmod(p, PAIRS)
                served = slot_uses[p - 1] if p else []
                for use in served:
                    serve(use)
                if p + 1 < NP:
                    exps(p + 1)
                act.wait_ge(pt_full, 2 * p + 2)
                if p >= 4:
                    act.wait_ge(aux_full, weighed(p // 2 - 2))
                act.activation(probsT[:, (p // 2) % 2, 2 * (p % 2) + 1, :], bank[PT[1]][:, 0:L + P],
                               ACT.Copy).then_inc(pt_ev[1], 1)
                rotated = (1, 3) if b == 0 else (0, 1)
                if b + 1 < B and u in rotated:
                    high_parts(b + 1, rotated.index(u))
            for use in slot_uses[NP - 1] + slot_uses[NP] + last_uses:
                serve(use)

            def split_high(s, q):
                act.wait_ge(raw_in[s % RAW], raw_loaded(s))
                if s >= RING:
                    act.wait_ge(y_full, last_block(s - RING) + 1)
                c = quarter(q)
                act.activation(w_h[s % RING][:, c], w_raw[:, s % RAW, c], ACT.Copy).then_inc(w_high, 1)

            act.wait_ge(var_ready, 1)
            act.activation(std[:, :], mv[:, :, 1], ACT.Sqrt).then_inc(std_ready, 1)
            act.wait_ge(shift_ready, 1)
            for c in range(NT // 2):
                if c == 0:
                    for t in (2, 3):
                        act.activation(r1[:, t, :], r1[:, t, :], ACT.Identity, bias=shift[:, t:t + 1],
                                       scale=rstd[:, t:t + 1]).then_inc(x1_act, 1)
                act.wait_ge(x1T_full, c + 1)
                act.activation(x1T_h[:, :, c * 2 * P:(c + 1) * 2 * P],
                               bank[X1[c]][:, :].rearrange("p (k q) -> p k q", k=KE),
                               ACT.Copy).then_inc(x1T_high, 1)
            act.wait_ge(logitsT_full, 1)
            act.activation(lgT[:, 0:T // 2], bank[2][0:2 * NX, :], ACT.Copy).then_inc(lgT_act, 1)
            act.wait_ge(top_ready, 1)
            act.activation(score[:, :], top[:, :], ACT.Sigmoid).then_inc(score_ready, 1)

            def silu(n, f):
                i = n * KF + f
                act.wait_ge(gu_full, i + 1)
                if i >= 2:
                    act.wait_ge(h_ready, i - 1)
                act.activation(gate[:, i % 2, :], bank[4 + i % 4][:, 0:CAP], ACT.Silu).then_inc(gate_ready, 1)

            def h_split(n, f):
                i = n * KF + f
                act.wait_ge(h_ready, i + 1)
                if n >= 2:
                    act.wait_ge(y_full, n - 1)
                act.activation(hT_h[:, n % 2, f, :], hT[:, i % 2, :], ACT.Copy).then_inc(h_high, 1)

            def xs_high(e):
                act.wait_ge(xsT_full, e + 1)
                if e >= 2:
                    act.wait_ge(gu_full, (SH1 + e - 1) * KF)
                act.activation(xsT_h[:, e % 2, :, :], bank[2 + e % 2][:, :].rearrange("p (k q) -> p k q", k=KE),
                               ACT.Copy).then_inc(xsT_high, 1)

            def ys_copy(e):
                n = SH1 + e
                act.wait_ge(y_full, n + 1)
                if e >= 2:
                    act.wait_ge(ys_out[e % 2], 16 * (e // 2))
                act.activation(ys[:, e % 2, :, :].rearrange("p t d -> p (t d)"), bank[n % 2][:, :],
                               ACT.Copy).then_inc(ys_ready, 1)

            for n in range(NB):
                for f in range(KF):
                    silu(n, f)
                    if f:
                        h_split(n, f - 1)
                    if f == 1:
                        if split_with(n) and not rows_late(n):
                            for q in range(4):
                                split_high(split_with(n), q)
                        if SH1 <= n - 1 < SH2:
                            ys_copy(n - 1 - SH1)
                        if SH1 < n + 1 < SH2:
                            xs_high(n + 1 - SH1)
                h_split(n, KF - 1)
                if n + 1 == SH1:
                    for q in range(4):
                        split_high(split_with(n), q)
                    xs_high(0)
                    n_over_act = read_over(act)
            with act.If(n_over_act > 0):
                with act.Fori(0, NX * CHUNKS) as i:
                    for f in range(KF):
                        act.wait_ge(o_gu, i * KF + f + 1)
                        act.wait_ge(o_h, i * KF + f + 1)
                        act.activation(gate[:, 0, :], bank[4][:, 0:CAP], ACT.Silu).then_inc(o_gate, 1)
            act.wait_ge(var2, 1)
            act.activation(std[:, 0:NT - TT], mv[:, 0:NT - TT, 1], ACT.Sqrt).then_inc(std2, 1)
            act.wait_ge(shift2_ready, 1)
            for t in range(TT, NT - TT):
                act.activation(back[:, t, :], y_sh[:, t, :], ACT.Identity, bias=shift[:, t:t + 1],
                               scale=rstd[:, t:t + 1]).then_inc(done_act, 1)
            act.wait_ge(var2, 2)
            act.activation(std[:, NT - TT:], mv[:, NT - TT:, 1], ACT.Sqrt).then_inc(std2, 1)

        @block.vector
        def _(dve):
            links = [0]

            def link(ins):
                links[0] += 1
                ins.then_inc(dve_link, 1)
                dve.wait_ge(dve_link, links[0])

            def serve(use):
                kind, b, i = use
                bk = aux(use)
                if kind == "proj":
                    n = b * TT + i
                    dve.wait_ge(aux_full, use_at[use] + 1)
                    if b:
                        dve.wait_ge(v_ready, n - TT + 1)
                    dve.tensor_tensor(qkv[:, i, :], bk[:, 0:NQKV], bias_s[:, :], ALU.add).then_inc(rope_in, 1)
                    dve.wait_ge(rope_in, n + 1)
                    dve.tensor_tensor(rot_c[:, i, :, :], qkv[:, i, 0:HR * D].rearrange("p (h d) -> p h d", h=HR),
                                      cos_s[:, i, :].unsqueeze(1).broadcast_to((P, HR, D)), ALU.mult).then_inc(rope_cos, 1)
                elif kind == "qT" and i % 2 == 1:
                    dve.wait_ge(aux_full, use_at[use] + 1)
                    dve.tensor_copy(q4T[:, b % 2, 4:8, (i // 2) * P:(i // 2 + 1) * P],
                                    bk[:, :].rearrange("p (a q) -> p a q", a=4)).then_inc(qT_dve, 1)
                elif kind == "otr":
                    dve.wait_ge(aux_full, use_at[use] + 1)
                    heads = bk[:, :].rearrange("p (h d) -> p h d", d=2 * D)
                    if b and i == 0:
                        dve.wait_ge(aux_full, use_at[("onT", b - 1, 0)] + 1)
                    link(dve.reciprocal(rdenom[:, i, :].unsqueeze(2), heads[:, :, D:D + 1]))
                    dve.tensor_tensor(on[:, i, :, :], heads[:, :, 0:D],
                                      rdenom[:, i, :].unsqueeze(2).broadcast_to((P, HQ, D)),
                                      ALU.mult).then_inc(on_ready, 1)
                elif kind == "wo":
                    dve.wait_ge(aux_full, use_at[use] + 1)
                    dve.wait_ge(ld_r, 32)
                    a, z = b * TT + tiles_of(use)[0], b * TT + tiles_of(use)[-1] + 1
                    dve.tensor_tensor(r1[:, a:z, :], bk[:, 0:(z - a) * E].rearrange("p (t e) -> p t e", e=E),
                                      r1[:, a:z, :], ALU.add).then_inc(r1_ready, 1)

            def row_moments(use):
                dve.wait_ge(r1_ready, outputs_done(use))
                rows = [use[1] * TT + t for t in tiles_of(use)]
                for t in rows:
                    last = dve.bn_stats(stats[:, t, :], r1[:, t, :])
                link(last)
                for t in rows:
                    last = dve.bn_aggr(mv[:, t, :], stats[:, t, :])
                return last

            def maxes(p):
                b, u = divmod(p, PAIRS)
                dve.wait_ge(scores_full, p + 1)
                s = SCORES[p % 2]
                dve.reduce_max(negmax[:, b, 1, 2 * u:2 * u + 2], bank[s][:, :].rearrange("p (h k) -> p h k", h=2),
                               AX.X, negate=True).then_inc(max_ready, 1)
                dve.reduce_max(negmax[:, b, 0, 2 * u:2 * u + 2],
                               bank[s + 1][:, 0:2 * P].rearrange("p (h k) -> p h k", h=2),
                               AX.X, negate=True).then_inc(max_ready, 1)

            dve.memset(idle[:, :], 0.0).then_inc(warm_ready, 1)
            dve.wait_ge(ld_c, 16 * 5)
            for use in first_uses:
                serve(use)
                if use[0] == "proj":
                    t = use[2]
                    dve.wait_ge(rope_cos, t + 1)
                    dve.wait_ge(rope_sin, 2 * t + 2)
                    dve.tensor_tensor(rot[:, t, :, :], rot_c[:, t, :, :],
                                      rot_s[:, t, :, :, :].rearrange("p h s d -> p h (s d)"),
                                      ALU.add).then_inc(rope_sum, 1)
                if use == ("proj", 0, TT - 1):
                    for t in range(TT):
                        dve.wait_ge(q_high, 2 * t + 2)
                        dve.tensor_tensor(q4[:, t, :, 2:4, :],
                                          rot[:, t, 0:HQ, :].unsqueeze(2).broadcast_to((P, HQ, 2, D)),
                                          q4[:, t, :, 0:2, :].bitcast(FP32), ALU.subtract).then_inc(q_low, 1)
                    dve.tensor_copy(ident_b, ident).then_inc(masks_ready, 1)
                    dve.tensor_copy(mask2, mask_f.unsqueeze(1).broadcast_to((P, 2, P))).then_inc(masks_ready, 1)
                    dve.tensor_scalar(earlier, mask_f, 0.0, None, ALU.is_lt).then_inc(masks_ready, 1)
            maxes(0)
            for use in second_uses:
                serve(use)
            maxes(1)
            for p in range(NP):
                served = slot_uses[p - 1] if p else []
                for use in served:
                    serve(use)
                dve.wait_ge(pt_full, 2 * p + 1)
                if p >= 4:
                    dve.wait_ge(aux_full, weighed(p // 2 - 2))
                dve.tensor_copy(probsT[:, (p // 2) % 2, 2 * (p % 2), :],
                                bank[PT[0]][:, 0:L + P]).then_inc(pt_ev[0], 1)
                if p + 2 < NP:
                    maxes(p + 2)
                for use in served:
                    if use[0] == "wo" and use[1] < B - 2:
                        row_moments(use)
                if p == PAIRS:
                    dve.wait_ge(ld_r, 32)
                    link(dve.tensor_copy(rw_r[:, :, 0, :], rw_s[:, :, :]))
                    dve.tensor_tensor(rw_r[:, :, 1, :], rw_s[:, :, :], rw_r[:, :, 0, :].bitcast(FP32),
                                      ALU.subtract).then_inc(rw_ready, 1)
            for use in slot_uses[NP - 1] + slot_uses[NP] + last_uses:
                if use == ("wo", B - 1, 0):
                    row_moments(("wo", B - 2, 0))
                serve(use)
                if use[0] == "wo" and use[1] == B - 1:
                    last = row_moments(use)
            link(last)
            dve.tensor_scalar(mv[:, :, 1], mv[:, :, 1], EPS, None, ALU.add).then_inc(var_ready, 1)
            dve.wait_ge(std_ready, 1)
            link(dve.reciprocal(rstd[:, :], std[:, :]))

            def normalise(t):
                dve.tensor_scalar(r1[:, t, :], r1[:, t, :], mv[:, t, 0:1], rstd[:, t:t + 1],
                                  ALU.subtract, ALU.mult).then_inc(x1_ready, 1)

            normalise(0)
            dve.scalar_tensor_tensor(out=shift[:, :], in0=mv[:, :, 0], scalar=-1.0, in1=rstd[:, :],
                                     op0=ALU.mult, op1=ALU.mult).then_inc(shift_ready, 1)
            for t in (1, 4, 5, 6, 7):
                normalise(t)
            for c in range(NT // 2):
                dve.wait_ge(x1T_high, c + 1)
                cols = slice(c * 2 * P, (c + 1) * 2 * P)
                dve.tensor_tensor(x1T_l[:, :, cols], bank[X1[c]][:, :].rearrange("p (k q) -> p k q", k=KE),
                                  x1T_h[:, :, cols].bitcast(FP32), ALU.subtract).then_inc(x1T_low, 1)
            dve.wait_ge(logitsT_full, 2)
            dve.tensor_copy(lgT[:, T // 2:], bank[3][0:2 * NX, :]).then_inc(lgT_dve, 1)

            def split_low(s, q):
                dve.wait_ge(w_high, split_count(s, q))
                c = quarter(q, 0)
                dve.tensor_tensor(w_l[s % RING][:, c], w_raw[:, s % RAW, c],
                                  w_h[s % RING][:, c].bitcast(FP32), ALU.subtract).then_inc(w_low_dve, 1)

            dve.wait_ge(logits_full, 1)
            link(dve.tensor_copy(lg[:, :, :], bank[0][:, 0:NT * NX].rearrange("p (t e) -> p t e", t=NT)))
            dve.reduce_max(top[:, :], lg[:, :, :], AX.X).then_inc(top_ready, 1)
            dve.wait_ge(top_ready, 1)
            link(dve.tensor_tensor(pick[:, :, :], lg[:, :, :], top[:, :].unsqueeze(2).broadcast_to((P, NT, NX)),
                                   ALU.is_lt))
            link(dve.scalar_tensor_tensor(out=place[:, :, :], in0=pick[:, :, :], scalar=float(NX),
                                          in1=expert_no.unsqueeze(1).broadcast_to((P, NT, NX)),
                                          op0=ALU.mult, op1=ALU.add))
            link(dve.tensor_reduce(first[:, :], place[:, :, :], AX.X, ALU.min))
            fb = first[:, :].unsqueeze(2).broadcast_to((P, NT, NX))
            xb = expert_no.unsqueeze(1).broadcast_to((P, NT, NX))
            dve.tensor_tensor(onehot_b[:, :, :], xb, fb, ALU.is_equal).then_inc(onehot_ready, 1)
            dve.tensor_tensor(onehot[:, :, :], xb, fb, ALU.is_equal).then_inc(onehot_ready, 1)

            def scale_rows(t):
                dve.tensor_scalar(x1s[:, t, :], r1[:, t, :], score[:, t:t + 1], None, ALU.mult).then_inc(scaled, 1)

            dve.wait_ge(score_ready, 1)
            for t in range(2):
                scale_rows(t)
            dve.wait_ge(onehot_ready, 2)
            dve.wait_ge(rank_full, 1)
            link(dve.tensor_tensor(place[:, :, :], bank[3][:, 0:NT * NX].rearrange("p (t e) -> p t e", t=NT),
                                   onehot[:, :, :], ALU.mult))
            link(dve.reduce_sum(rank[:, :], place[:, :, :], AX.X))
            dve.tensor_scalar(over[:, :], rank[:, :], float(CAP), None, ALU.is_ge)
            link(dve.scalar_tensor_tensor(out=slot_f[:, :], in0=first[:, :], scalar=float(CAP),
                                          in1=rank[:, :], op0=ALU.mult, op1=ALU.add))
            link(dve.scalar_tensor_tensor(out=slot_f[:, :], in0=over[:, :], scalar=float(NSLOT),
                                          in1=slot_f[:, :], op0=ALU.mult, op1=ALU.add))
            dve.tensor_copy(slot_u[:, :], slot_f[:, :]).then_inc(slot_ready, 1)
            for t in range(2, NT):
                scale_rows(t)
            dve.tensor_copy(over_b[:, :], over[:, :]).then_inc(over_ready, 1)
            dve.tensor_tensor(over_mask[:, :, :], onehot[:, :, :],
                              over[:, :].unsqueeze(2).broadcast_to((P, NT, NX)), ALU.mult)

            def count_over():
                dve.wait_ge(over_full, 1)
                link(dve.reduce_sum(n_over_f[:, :], bank[3][:, NT * NX:NT * NX + NT], AX.X))
                dve.tensor_copy(n_over[:, :], n_over_f[:, :]).then_inc(n_over_ready, 1)

            def h_product(n, f):
                i = n * KF + f
                dve.wait_ge(gate_ready, i + 1)
                if i >= 2:
                    dve.wait_ge(h_high, i - 1)
                    dve.wait_ge(h_low, i - 1)
                dve.tensor_tensor(hT[:, i % 2, :], bank[4 + i % 4][:, CAP:2 * CAP], gate[:, i % 2, :],
                                  ALU.mult).then_inc(h_ready, 1)

            def h_rest(n, f):
                i = n * KF + f
                dve.wait_ge(h_high, i + 1)
                dve.tensor_tensor(hT_l[:, n % 2, f, :], hT[:, i % 2, :], hT_h[:, n % 2, f, :].bitcast(FP32),
                                  ALU.subtract).then_inc(h_low, 1)

            def xs_low(e):
                dve.wait_ge(xsT_high, e + 1)
                dve.tensor_tensor(xsT_l[:, e % 2, :, :], bank[2 + e % 2][:, :].rearrange("p (k q) -> p k q", k=KE),
                                  xsT_h[:, e % 2, :, :].bitcast(FP32), ALU.subtract).then_inc(xsT_low, 1)

            def chunk(a, c):
                return a[:, c * TT:(c + 1) * TT, :]

            def add_shared(n):
                c = chunk_of(n)
                dve.wait_ge(y_full, n + 1)
                if c >= SH1:
                    dve.wait_ge(joined, (c - SH1 + 1) * TT)
                dve.tensor_tensor(chunk(y_sh, c), bank[n % 2][:, :].rearrange("p (t e) -> p t e", t=TT),
                                  chunk(y_sh if c >= SH1 else r1, c), ALU.add).then_inc(y_sh_ready, 1)

            def add_routed(c):
                for t in range(c * TT, (c + 1) * TT):
                    dve.wait_ge(got[t], 16)
                    last = dve.tensor_tensor(y_sh[:, t, :], y_sh[:, t, :], back[:, t, :], ALU.add)
                return last

            def moments(c, link=link):
                for t in range(c * TT, (c + 1) * TT):
                    last = dve.bn_stats(stats[:, t, :], y_sh[:, t, :])
                link(last)
                for t in range(c * TT, (c + 1) * TT):
                    last = dve.bn_aggr(mv[:, t, :], stats[:, t, :])
                return last

            for n in range(NB):
                for f in range(KF):
                    h_product(n, f)
                    if f:
                        h_rest(n, f - 1)
                    if n == 1 and f == 0:
                        count_over()
                    if f == 1:
                        if split_with(n) and not rows_late(n):
                            for q in range(4):
                                split_low(split_with(n), q)
                        if n and chunk_of(n - 1) is not None and not rows_late(n):
                            add_shared(n - 1)
                        if SH1 < n + 1 < SH2:
                            xs_low(n + 1 - SH1)
                h_rest(n, KF - 1)
                if n + 1 == SH1:
                    for q in range(4):
                        split_low(split_with(n), q)
                    add_shared(n - 1)
                    n_over_dve = read_over(dve)
                    xs_low(0)
            for c in range(CHUNKS - 1):
                if c < SH1:
                    link(add_routed(c))
                else:
                    add_shared(SH2 + c - SH1)
                    dve.wait_ge(y_sh_ready, c + 1)
                last = moments(c)
            link(last)
            with dve.If(n_over_dve > 0):
                dve.wait_ge(joined, NT - SH1 * TT)
                dve.sem_inc(o_h, 1)
                dve.sem_inc(o_sum, 1)
                with dve.Fori(0, NX) as e:
                    with dve.Fori(0, CHUNKS) as c:
                        i = e * CHUNKS + c
                        for t in range(TT):
                            dve.tensor_scalar(xs[:, 0, t, :],
                                              r1[:, bass.ds(c * TT + t, 1), :].rearrange("p a e -> p (a e)"),
                                              score[:, bass.ds(c * TT + t, 1)], None, ALU.mult
                                              ).then_inc(o_rows, 1)
                        dve.wait_ge(o_xT_full, i + 1)
                        dve.tensor_copy(xsT_o, bank[2][:, :].rearrange("p (k c) -> p k c", k=KE)
                                        ).then_inc(o_xT, 1)
                        for f in range(KF):
                            dve.wait_ge(o_gate, i * KF + f + 1)
                            dve.tensor_tensor(hT_o[:, f, :], bank[4][:, CAP:2 * CAP], gate[:, 0, :],
                                              ALU.mult).then_inc(o_h, 1)
                        dve.wait_ge(o_y, i + 1)
                        for t in range(TT):
                            rows = y_sh[:, bass.ds(c * TT + t, 1), :].rearrange("p a e -> p (a e)")
                            last = dve.scalar_tensor_tensor(
                                out=rows, in0=bank[0][:, t * E:(t + 1) * E],
                                scalar=over_mask[:, bass.ds(c * TT + t, 1), bass.ds(e, 1)].rearrange("p a b -> p (a b)"),
                                in1=rows, op0=ALU.mult, op1=ALU.add)
                        last.then_inc(o_sum, 1)
                        dve.wait_ge(o_sum, i + 2)
                over_links = [0]

                def over_link(ins):
                    over_links[0] += 1
                    ins.then_inc(o_link, 1)
                    dve.wait_ge(o_link, over_links[0])

                for c in range(CHUNKS - 1):
                    last = moments(c, over_link)
                over_link(last)
            for part, tiles in enumerate((range(NT - TT), range(NT - TT, NT))):
                a, z = tiles[0], tiles[-1] + 1
                if part:
                    add_shared(NB - 1)
                    dve.wait_ge(y_sh_ready, CHUNKS)
                    link(moments(CHUNKS - 1))
                dve.tensor_scalar(mv[:, a:z, 1], mv[:, a:z, 1], EPS, None, ALU.add).then_inc(var2, 1)
                dve.wait_ge(std2, part + 1)
                link(dve.reciprocal(rstd[:, a:z], std[:, a:z]))
                if part == 0:
                    dve.scalar_tensor_tensor(out=shift[:, a:z], in0=mv[:, a:z, 0], scalar=-1.0, in1=rstd[:, a:z],
                                             op0=ALU.mult, op1=ALU.mult).then_inc(shift2_ready, 1)
                for t in tiles if part else range(TT):
                    dve.tensor_scalar(back[:, t, :], y_sh[:, t, :], mv[:, t, 0:1], rstd[:, t:t + 1],
                                      ALU.subtract, ALU.mult).then_inc(done, 1)

        @block.tensor
        def _(pe):
            def scores(p):
                b, u = divmod(p, PAIRS)
                kv = u // (PAIRS // HKV)
                s = SCORES[p % 2]
                if p >= 2:
                    pe.wait_ge(exp_ready, 4 * (p - 1))
                if u == 0:
                    pe.wait_ge(qT_act, 2 * b + 2)
                    pe.wait_ge(kT_ready, 2 * b + 2)
                if u == PAIRS // 2:
                    pe.wait_ge(qT_dve, 2 * b + 2)
                pe.matmul(bank[s][:, :], q4T[:, b % 2, u, P:L],
                          kbd[:, b % 2, kv, :, :].rearrange("p h k -> p (h k)"), start=True, stop=False)
                pe.matmul(bank[s][:, :].rearrange("p (h k) -> p h k", h=2)[:, :, P:L], ident_b, mask2,
                          start=False, stop=True)
                pe.matmul(bank[s + 1][:, 0:2 * P].rearrange("p (h k) -> p h k", h=2), q4T[:, b % 2, u, 0:P],
                          kbd[:, b % 2, kv, :, 0:P], start=True, stop=False)
                pe.matmul(bank[s + 1][:, 0:2 * P].rearrange("p (h k) -> p h k", h=2), ident_b, mask2,
                          start=False, stop=True).then_inc(scores_full, 1)

            def transpose_probs(p, j):
                pe.wait_ge(exp_ready, 4 * p + 2 * j + 2)
                if p:
                    pe.wait_ge(pt_ev[j], p)
                pr = probs[:, p % 2, j, :]
                for dst, src in ((0, L), (P, 0), (2 * P, P)):
                    last = pe.transpose(bank[PT[j]][:, dst:dst + P], pr[:, src:src + P], ident)
                last.then_inc(pt_full, 1)

            def wait_emptied(use):
                kind, b, i = use
                if kind == "proj":
                    pe.wait_ge(rope_in, b * TT + i + 1)
                elif kind == "qT":
                    pe.wait_ge((qT_act, qT_dve)[i % 2], b * 2 + i // 2 + 1)
                elif kind == "kT":
                    pe.wait_ge(kT_ready, 2 * b + 2)
                elif kind == "pv":
                    pe.wait_ge(o_ev, b * GB + i + 1)
                elif kind == "otr":
                    pe.wait_ge(on_ready, b * TT + i + 1)
                elif kind == "onT":
                    pe.wait_ge(onT_ready, outputs_done(use))
                else:
                    pe.wait_ge(r1_ready, outputs_done(use))

            def fill_aux(use):
                kind, b, i = use
                if use_at[use] >= 2:
                    wait_emptied(uses[use_at[use] - 2])
                bk = aux(use)
                if kind == "pv":
                    g = b * GB + i
                    kv = i // (GB // HKV)
                    pe.wait_ge(pt_ev[0], 2 * g + 2)
                    pe.wait_ge(pt_ev[1], 2 * g + 2)
                    if i == 0:
                        pe.wait_ge(v_ready, TT * (b + 1))
                    for k, src, dst in ((0, 0, 0), (1, L, P)):
                        for j in range(4):
                            last = pe.matmul(bk[32 * j:32 * j + 32, dst:L], v_s[:, b % 3, k, kv, :],
                                             probsT[:, g % 2, j, src:src + L - dst], start=(k == 0), stop=(k == 1))
                elif kind == "proj":
                    for k in range(KE):
                        last = pe.matmul(bk[:, 0:NQKV], xT_s[:, k, (b * TT + i) * P:(b * TT + i + 1) * P],
                                         wqkv_s[:, k, :], start=(k == 0), stop=(k == KE - 1))
                elif kind == "qT":
                    t, half = divmod(i, 2)
                    pe.wait_ge(q_low, 2 * (b * TT + t) + 2)
                    for a in range(4):
                        h = 2 * (4 * half + a)
                        last = pe.transpose(bk[:, a * P:(a + 1) * P],
                                            q4[:, t, h:h + 2, :, :].bitcast(FP32).rearrange("p h s d -> p (h s d)"),
                                            ident)
                elif kind == "kT":
                    pe.wait_ge(q_low, 2 * (b * TT + TT - 1) + 2)
                    for t in range(TT):
                        for h in range(HKV):
                            at2 = t * HKV + h
                            last = pe.transpose(bk[:, at2 * P:(at2 + 1) * P],
                                                k4[:, t, h, :, :, :].bitcast(FP32).rearrange("p a s d -> p (a s d)"),
                                                ident)
                elif kind == "otr":
                    pe.wait_ge(o_ev, GB * (b + 1))
                    for g in range(GB):
                        last = pe.transpose(bk[:, g * P:(g + 1) * P], oT_s[:, b % 2, g, i * P:(i + 1) * P], ident)
                elif kind == "onT":
                    pe.wait_ge(on_ready, TT * b + tiles_of(use)[-1] + 1)
                    for at, t in enumerate(tiles_of(use)):
                        for k in range(KE):
                            last = pe.transpose(bk[:, at * E + k * P:at * E + (k + 1) * P],
                                                on[:, t, 8 * k:8 * k + 8, :].rearrange("p h d -> p (h d)"), ident)
                else:
                    pe.wait_ge(onT_ready, outputs_done(use))
                    for at, t in enumerate(tiles_of(use)):
                        for k in range(KE):
                            last = pe.matmul(bk[:, at * E:(at + 1) * E], onT_s[:, t, k, :], wo_s[:, k, :],
                                             start=(k == 0), stop=(k == KE - 1))
                last.then_inc(aux_full, 1)

            def keep_warm(wait):
                for _ in range(WARM[wait]):
                    pe.matmul(bank[3][:, :], idle[:, 0:P], idle[:, :], start=True, stop=True)

            pe.wait_ge(warm_ready, 1)
            keep_warm("loads")
            pe.wait_ge(ld_x, 32)
            for use in first_uses:
                if use == ("kT", 0, 0):
                    keep_warm("rotation")
                if use[0] == "kT":
                    pe.wait_ge(ld_c, 16 * 5)
                fill_aux(use)
            pe.wait_ge(init, 4)
            pe.wait_ge(masks_ready, 3)
            keep_warm("first queries")
            scores(0)
            for use in second_uses:
                fill_aux(use)
            scores(1)
            pe.wait_ge(ld_w, 32)
            for p in range(NP):
                transpose_probs(p, 0)
                if p + 2 < NP:
                    scores(p + 2)
                transpose_probs(p, 1)
                for use in slot_uses[p]:
                    fill_aux(use)
            for use in slot_uses[NP] + last_uses:
                fill_aux(use)
            keep_warm("layer norm")

            for c in range(NT // 2):
                if c == 1:
                    pe.wait_ge(x1_act, 2)
                else:
                    pe.wait_ge(x1_ready, 2 * (c + 1 if c == 0 else c))
                for k in range(KE):
                    for t in range(2):
                        last = pe.transpose(bank[X1[c]][:, (2 * k + t) * P:(2 * k + t + 1) * P],
                                            r1[:, 2 * c + t, k * P:(k + 1) * P], ident)
                last.then_inc(x1T_full, 1)
            pe.wait_ge(rw_ready, 1)
            for half in range(2):
                cols = slice(half * T // 2, (half + 1) * T // 2)
                pe.wait_ge(x1T_low, (half + 1) * NT // 4)
                for k in range(KE):
                    pe.matmul(bank[2 + half][0:2 * NX, :], rw_r[:, k, :, :].rearrange("p s e -> p (s e)"),
                              x1T_h[:, k, cols], start=(k == 0), stop=False)
                for k in range(KE):
                    last = pe.matmul(bank[2 + half][0:NX, :], rw_r[:, k, 0, :], x1T_l[:, k, cols],
                                     start=False, stop=(k == KE - 1))
                last.then_inc(logitsT_full, 1)
            for t in range(NT):
                if t == 0:
                    pe.wait_ge(lgT_act, 1)
                if t == NT // 2:
                    pe.wait_ge(lgT_dve, 1)
                last = pe.matmul(bank[0][:, t * NX:(t + 1) * NX], lgT[:, t * P:(t + 1) * P], sum_parts,
                                 start=True, stop=True)
            last.then_inc(logits_full, 1)

            def products(n):
                if chunk_of(n) is not None:
                    c = slice(chunk_of(n) * CAP, (chunk_of(n) + 1) * CAP)
                    return [(x1T_h[:, k, c], x1T_l[:, k, c]) for k in range(KE)]
                e = n - SH1
                return [(xsT_h[:, e % 2, k, :], xsT_l[:, e % 2, k, :]) for k in range(KE)]

            def weights(s, q):
                if s < EARLY:
                    pe.wait_ge(early_low, 4 * s + q + 1)
                else:
                    pe.wait_ge(w_low_dve, split_count(s, q))
                    pe.wait_ge(w_low_pool, split_count(s, q))

            def gate_up(n, f):
                i = n * KF + f
                par = set_of(n) % RING
                if f == 0:
                    weights(set_of(n), 2)
                    if chunk_of(n) is None:
                        pe.wait_ge(xsT_low, n - SH1 + 1)
                if i >= 4:
                    pe.wait_ge(h_ready, i - 3)
                xt = products(n)
                for up in range(2):
                    o = bank[4 + i % 4][:, up * CAP:(up + 1) * CAP]
                    for k in range(KE):
                        pe.matmul(o, gu(par, True, f, k, up), xt[k][0], start=(k == 0), stop=False)
                        pe.matmul(o, gu(par, True, f, k, up), xt[k][1], start=False, stop=False)
                        last = pe.matmul(o, gu(par, False, f, k, up), xt[k][0], start=False, stop=(k == KE - 1))
                last.then_inc(gu_full, 1)

            def down_rows(n, tiles=range(TT)):
                par = set_of(n) % RING
                pe.wait_ge(h_low, (n + 1) * KF)
                weights(set_of(n), 3)
                if n >= 2:
                    if chunk_of(n - 2) is None:
                        pe.wait_ge(ys_ready, n - 1 - SH1)
                    else:
                        pe.wait_ge(y_sh_ready, chunk_of(n - 2) + 1)
                for t in tiles:
                    o = bank[n % 2][:, t * E:(t + 1) * E]
                    c = slice(t * P, (t + 1) * P)
                    for f in range(KF):
                        pe.matmul(o, hT_h[:, n % 2, f, c], down(par, True, f), start=(f == 0), stop=False)
                        pe.matmul(o, hT_h[:, n % 2, f, c], down(par, False, f), start=False, stop=False)
                        last = pe.matmul(o, hT_l[:, n % 2, f, c], down(par, True, f), start=False,
                                         stop=(f == KF - 1))
                if TT - 1 in tiles:
                    last.then_inc(y_full, 1)

            def rows_T(e):
                pe.wait_ge(xs_in[e % 2], 16 * (e // 2 + 1))
                if e >= 2:
                    pe.wait_ge(xsT_low, e - 1)
                for k in range(KE):
                    for t in range(TT):
                        last = pe.transpose(bank[2 + e % 2][:, k * CAP + t * P:k * CAP + (t + 1) * P],
                                            xs[:, e % 2, t, k * P:(k + 1) * P], ident)
                last.then_inc(xsT_full, 1)

            for n in range(NB):
                for f in range(KF):
                    gate_up(n, f)
                    if n == 0 and f == 0:
                        pe.wait_ge(onehot_ready, 1)
                        o = bank[3][:, 0:NT * NX].rearrange("p (t e) -> p t e", t=NT)
                        pe.matmul(o, earlier, onehot_b[:, :, :], start=True, stop=False)
                        for s in range(1, NT):
                            last = pe.matmul(o[:, s:NT, :], ones_b, onehot_b[:, 0:NT - s, :], start=False,
                                             stop=(s == NT - 1))
                        last.then_inc(rank_full, 1)
                    if n == 0 and f == 3:
                        pe.wait_ge(over_ready, 1)
                        pe.matmul(bank[3][:, NT * NX:NT * NX + NT], ones_b, over_b[:, :], start=True,
                                  stop=True).then_inc(over_full, 1)
                    if f == 1 and n and n != SH1 and not rows_late(n):
                        down_rows(n - 1)
                    if f == 1 and SH1 < n + 1 < SH2:
                        rows_T(n + 1 - SH1)
                if rows_late(n):
                    down_rows(n - 1)
                if n + 1 == SH1:
                    down_rows(n, [0])
                    rows_T(0)
                    down_rows(n, [1])
                    n_over_pe = read_over(pe)
            down_rows(NB - 1)
            with pe.If(n_over_pe > 0):
                with pe.Fori(0, NX) as e, pe.Fori(0, CHUNKS) as c:
                    i = e * CHUNKS + c
                    pe.wait_ge(o_rows, i * TT + TT)
                    for k in range(KE):
                        for t in range(TT):
                            last = pe.transpose(bank[2][:, k * CAP + t * P:k * CAP + (t + 1) * P],
                                                xs[:, 0, t, k * P:(k + 1) * P], ident)
                    last.then_inc(o_xT_full, 1)
                    pe.wait_ge(o_xT, i + 1)
                    pe.wait_ge(o_w, e * 32 + 32)
                    g, d = w_raw[:, 0, part_of(0)], w_raw[:, 0, part_of(1)]
                    g, d = g.rearrange("p (k n) -> p k n", k=KE), d.rearrange("p (f n) -> p f n", f=KF)
                    for f in range(KF):
                        pe.wait_ge(o_h, i * KF + f + 1)
                        for up in range(2):
                            for k in range(KE):
                                n = up * F + f * P
                                last = pe.matmul(bank[4][:, up * CAP:(up + 1) * CAP], g[:, k, n:n + P],
                                                 xsT_o[:, k, :], start=(k == 0), stop=(k == KE - 1))
                        last.then_inc(o_gu, 1)
                    pe.wait_ge(o_h, i * KF + KF + 1)
                    for t in range(TT):
                        for f in range(KF):
                            last = pe.matmul(bank[0][:, t * E:(t + 1) * E], hT_o[:, f, t * P:(t + 1) * P],
                                             d[:, f, :], start=(f == 0), stop=(f == KF - 1))
                    last.then_inc(o_y, 1)


def constants():
    half = np.arange(HALF, dtype=np.float32) / np.float32(HALF)
    inv = (np.float32(THETA) ** (-half)).astype(np.float32)
    ang = np.arange(L, dtype=np.float32)[:, None] * inv[None, :]
    cos, sin = np.cos(ang).astype(np.float32), np.sin(ang).astype(np.float32)
    eye = np.eye(P, dtype=np.float32)
    cf = np.concatenate([eye, np.tile(np.arange(NX, dtype=np.float32), (P, 1)),
                         np.tile(np.eye(NX, dtype=np.float32), (P // NX, 1))], 1)
    k, q = np.arange(P)[None, :], np.arange(P)[:, None]
    mask = np.where(k > q, np.float32(MASKED), np.float32(0))
    return np.concatenate([cos, cos], 1), np.concatenate([-sin, sin], 1), cf, mask


def kernel(**inputs):
    import concourse.bacc as bacc
    from concourse.bass_utils import run_bass_kernel_spmd

    a = {n: np.asarray(v) for n, v in inputs.items()}
    x = a["L0_attn_x"].reshape(T, E)
    cos, sin, cf, mask = constants()
    arrays = {
        "x": x,
        "xT": x.T,
        "wqkvT": np.concatenate([a["L0_attn_wq"], a["L0_attn_wk"], a["L0_attn_wv"]], 0).T,
        "bqkv": np.concatenate([a["L0_attn_bq"], a["L0_attn_bk"], a["L0_attn_bv"]])[None, :],
        "woT": a["L0_attn_wo"].T,
        "rwT": a["L0_ffn_router_w"].T,
        "wgu": a["L0_ffn_gate_up_proj"],
        "wd": a["L0_ffn_down_proj"],
        "swg": a["L0_ffn_shared_gate_w"],
        "swu": a["L0_ffn_shared_up_w"],
        "swd": a["L0_ffn_shared_down_w"],
        "cos": cos, "sin": sin, "cf": cf, "mask": mask,
    }
    arrays = {n: np.ascontiguousarray(v) for n, v in arrays.items()}
    nc = bacc.Bacc("TRN2", target_bir_lowering=False, num_devices=1)
    args = [nc.dram_tensor(n, v.shape, mybir.dt.from_np(v.dtype), kind="ExternalInput").ap()
            for n, v in arrays.items()]
    out = nc.dram_tensor("out", (T, E), FP32, kind="ExternalOutput").ap()
    program(nc, *args, out)
    r = run_bass_kernel_spmd(nc, [arrays], core_ids=[0])
    return r.results[0]["out"].reshape(B, L, E)
```
